# Optimizing a Trainium2 kernel written in Bass

```python
import numpy as np
import jax
import jax.numpy as jnp

def _softmax(x, axis=-1):
    return jax.nn.softmax(x, axis=axis)

def _gelu(x):
    return jax.nn.gelu(x, approximate=True)

def _silu(x):
    return jax.nn.silu(x)

def _sigmoid(x):
    return jax.nn.sigmoid(x)

def _layernorm(x, axis=-1, eps=1e-05):
    m = jnp.mean(x, axis=axis, keepdims=True)
    v = jnp.var(x, axis=axis, keepdims=True)
    return (x - m) / jnp.sqrt(v + eps)

def _scatter_add(tgt, idx, src, axis=0):
    return tgt.at[idx].add(src)

def _segment_sum(src, seg, n):
    return jax.ops.segment_sum(src, seg, n)
kernel_name = 'mk_xattn_ffn_d1_seqx_r4_246e97'

def setup_inputs(seed: int=0):
    np.random.seed(seed)
    _w = jnp.asarray

    def _rec_inputs():
        import jax
        import jax.numpy as jnp
        _rk = jax.random.key(seed)
        x = -0.0003929 + 0.9999 * jax.random.normal(jax.random.fold_in(_rk, 1), (2, 1024, 256), jnp.float32)
        _lenS = 1024 - jax.random.randint(jax.random.fold_in(_rk, 7), (2,), 0, max(1, 1024 // 4) + 1, jnp.int32)
        _lenS2 = 77 - jax.random.randint(jax.random.fold_in(_rk, 8), (2,), 0, max(1, 77 // 4) + 1, jnp.int32)
        _ctx_1024P = jax.random.normal(jax.random.fold_in(_rk, 11), (2, 16, 256), jnp.float32)
        _ctx_1024c = jax.random.dirichlet(jax.random.fold_in(_rk, 511), 0.3 * jnp.ones((16,), jnp.float32), (2, 77))
        _ctx_1024t = jnp.einsum('bsk,bkd->bsd', _ctx_1024c, _ctx_1024P)
        _ctx_1024t = _ctx_1024t * jax.lax.rsqrt(jnp.mean(jnp.square(_ctx_1024t)) + 1e-12) * 0.953939
        ctx_1024 = 2.81802e-05 + 1.00001 * (_ctx_1024t + 0.3 * jax.random.normal(jax.random.fold_in(_rk, 611), (2, 77, 256), jnp.float32))
        return (x, ctx_1024)
    x, ctx_1024 = _rec_inputs()

    def _L0_xattn_setup():
        import jax, jax.numpy as jnp
        import numpy as np
        B, LQ, LKV, D = (8, 512, 512, 256)
        key = jax.random.key(seed)
        k1, k2, k3, k4, k5, k6, k7 = jax.random.split(key, 7)
        s = 1.0 / np.sqrt(D)
        return {'query': jax.random.normal(k1, (B, LQ, D), jnp.float32), 'key': jax.random.normal(k2, (B, LKV, D), jnp.float32), 'value': jax.random.normal(k3, (B, LKV, D), jnp.float32), 'Wq': jax.random.uniform(k4, (D, D), jnp.float32, -s, s), 'bq': jax.random.uniform(k5, (D,), jnp.float32, -s, s), 'Wk': jax.random.uniform(k6, (D, D), jnp.float32, -s, s), 'bk': jax.random.uniform(k7, (D,), jnp.float32, -s, s), 'scale_factor': 32, 'dropout_p': 0}
    _L0_xattn_all = _L0_xattn_setup()
    _L0_xattn_in = {k: v for k, v in _L0_xattn_all.items() if k in ('Wq', 'bq', 'Wk', 'bk')}
    del _L0_xattn_all

    def _L0_ffn_setup():
        import jax, jax.numpy as jnp
        import numpy as np
        B, S, D, E, F = (2, 512, 256, 8, 1024)
        key = jax.random.key(seed)
        ks = jax.random.split(key, 4)
        return {'hidden_states': jax.random.normal(ks[0], (B, S, D), dtype=jnp.float32), 'Wr': jax.random.normal(ks[1], (D, E), dtype=jnp.float32) * (1.0 / np.sqrt(D)), 'W1': jax.random.normal(ks[2], (E, D, F), dtype=jnp.float32) * (1.0 / np.sqrt(D)), 'b1': jnp.zeros((E, F), dtype=jnp.float32), 'W2': jax.random.normal(ks[3], (E, F, D), dtype=jnp.float32) * (1.0 / np.sqrt(F)), 'b2': jnp.zeros((E, D), dtype=jnp.float32)}
    _L0_ffn_all = _L0_ffn_setup()
    _L0_ffn_in = {k: v for k, v in _L0_ffn_all.items() if k in ('Wr', 'W1', 'b1', 'W2', 'b2')}
    del _L0_ffn_all
    return {'x': x, 'ctx_1024': ctx_1024, 'L0_xattn_Wq': _L0_xattn_in['Wq'], 'L0_xattn_bq': _L0_xattn_in['bq'], 'L0_xattn_Wk': _L0_xattn_in['Wk'], 'L0_xattn_bk': _L0_xattn_in['bk'], 'L0_ffn_Wr': _L0_ffn_in['Wr'], 'L0_ffn_W1': _L0_ffn_in['W1'], 'L0_ffn_b1': _L0_ffn_in['b1'], 'L0_ffn_W2': _L0_ffn_in['W2'], 'L0_ffn_b2': _L0_ffn_in['b2']}

def reference(x, ctx_1024, L0_xattn_Wq, L0_xattn_bq, L0_xattn_Wk, L0_xattn_bk, L0_ffn_Wr, L0_ffn_W1, L0_ffn_b1, L0_ffn_W2, L0_ffn_b2):
    import jax
    import jax.numpy as jnp

    def _L0_xattn_ref(query, key, value, Wq, bq, Wk, bk, scale_factor, dropout_p):
        import jax, jax.numpy as jnp
        import numpy as np
        B, LQ, LKV, D = (8, 512, 512, 256)
        q = jnp.einsum('bld,ed->ble', query, Wq) + bq
        k = jnp.einsum('bld,ed->ble', key, Wk) + bk
        scores = jnp.einsum('bqd,bkd->bqk', q, k) / jnp.float32(scale_factor)
        attn = jax.nn.softmax(scores, axis=-1)
        return jnp.einsum('bqk,bkd->bqd', attn, value)

    def _L0_ffn_ref(hidden_states, Wr, W1, b1, W2, b2):
        import jax, jax.numpy as jnp
        import numpy as np
        B, S, D, E, F = (2, 512, 256, 8, 1024)
        b, s, d = hidden_states.shape
        e = Wr.shape[1]
        x = hidden_states.reshape(b * s, d)
        router_logits = x @ Wr
        router_probs = jax.nn.softmax(router_logits, axis=-1)
        expert_idx = jnp.argmax(router_probs, axis=-1)
        p_max = jnp.max(router_probs, axis=-1, keepdims=True)

        def expert_mlp(w1, bb1, w2, bb2):
            h = jax.nn.gelu(x @ w1 + bb1, approximate=False)
            return h @ w2 + bb2
        outs = jax.vmap(expert_mlp)(W1, b1, W2, b2)
        onehot = jax.nn.one_hot(expert_idx, e, dtype=x.dtype)
        next_states = jnp.einsum('te,etd->td', onehot, outs)
        out = p_max * next_states
        return out.reshape(b, s, d)
    x = x + _L0_xattn_ref(_layernorm(x, axis=-1), ctx_1024, ctx_1024, L0_xattn_Wq, L0_xattn_bq, L0_xattn_Wk, L0_xattn_bk, 32, 0)
    x = x + _L0_ffn_ref(_layernorm(x, axis=-1), L0_ffn_Wr, L0_ffn_W1, L0_ffn_b1, L0_ffn_W2, L0_ffn_b2)
    return x

_drawn_inputs = setup_inputs


def setup_inputs(seed=0):
    import zlib

    import numpy as np

    out = dict(_drawn_inputs(seed))
    spreads = {'L0_ffn_b1': (0.0, 0.352), 'L0_ffn_b2': (0.0, 0.1)}
    factors = {'L0_xattn_bq': 7.953, 'L0_xattn_bk': 8.0}
    for name, (base, spread) in spreads.items():
        noise = np.random.default_rng([zlib.crc32(name.encode()), seed]).standard_normal(out[name].shape)
        drawn = base * np.exp(spread * noise) if base else spread * noise
        out[name] = jnp.asarray(drawn.astype(out[name].dtype))
    for name, factor in factors.items():
        out[name] = (out[name] * factor).astype(out[name].dtype)
    return out
```

```python
from contextlib import ExitStack

import concourse.bass as bass
from concourse import mybir

ALU = mybir.AluOpType
ACT = mybir.ActivationFunctionType
AXX = mybir.AxisListType.X
F32 = mybir.dt.float32
F16 = mybir.dt.float16
I32 = mybir.dt.int32

P = 128
D = 256
KD = D // P
B, S = 2, 1024
CTX = 77
E, F = 8, 1024
FC = F // P
TOKENS = B * S
TILES = TOKENS // P
TPB = S // P
GT = 4
GROUPS = TILES // GT
SLOTS = (TOKENS + E * (P - 1)) // P
ST = SLOTS + 1
ROW = D + 4
MEAN, RSTD, PMAX = D, D + 1, D + 2
EPS = 1e-5
ATT_SCALE = 1.0 / 32.0
XS = 64.0
WS = 64.0
HS = 16.0
PIECE = 1024
PIECES = E * 4
RING = 4
FAR = 8192.0


def build(nc, x, ctx, wq, bq, wk, bk, wr, w1, b1, w2, b2, out):
    assert SLOTS >= E and (TOKENS + 1) < FAR
    with ExitStack() as stack:
        def sb(name, shape, dt=F32):
            return stack.enter_context(nc.sbuf_tensor(name, shape, dt))

        def sem(name):
            return stack.enter_context(nc.semaphore(name))

        scratch = nc.dram_tensor("token_rows", [TOKENS + 1, ROW], F32, kind="Internal").ap()

        w1_hi = sb("w1_hi", [P, E * KD * F], F16)
        w1_lo = sb("w1_lo", [P, E * KD * F], F16)
        w2_hi = sb("w2_hi", [P, E * FC * D], F16)
        w2_lo = sb("w2_lo", [P, E * FC * D], F16)
        stage = sb("stage", [P, RING, PIECE])
        b2_rep = sb("b2_rep", [P, E * D])
        b1_T = sb("b1_T", [P, E * FC])
        gathered = sb("gathered", [P, SLOTS * ROW])
        xn = [gathered[:, i * 1024:(i + 1) * 1024].rearrange("p (j d) -> p j d", j=GT) for i in range(2)]
        xnT = [gathered[:, (2 + i) * 1024:(3 + i) * 1024].rearrange("p (k n) -> p k n", k=KD) for i in range(2)]
        probs = gathered[:, 4096:4096 + GT * 80].rearrange("p (j c) -> p j c", j=GT)
        wq_sb = gathered[:, 4416:4928].rearrange("p (k d) -> p k d", k=KD)
        wk_sb = gathered[:, 4928:5440].rearrange("p (k d) -> p k d", k=KD)
        row_onehot = gathered[:, 4416:5440].bitcast(F16).rearrange("p (t r) -> p t r", t=TILES)
        wkT = gathered[:, 5440:5952].rearrange("p (k d) -> p k d", k=KD)
        rows = sb("rows", [P, TILES, ROW])
        rows_flat = rows[:, :, :].rearrange("p t r -> p (t r)")
        h = [rows_flat[:, i * 1024:(i + 1) * 1024] for i in range(2)]
        h_hi = [rows_flat[:, 2048 + i * 512:2560 + i * 512].bitcast(F16) for i in range(2)]
        h_lo = [rows_flat[:, 3072 + i * 512:3584 + i * 512].bitcast(F16) for i in range(2)]

        ident = sb("ident", [P, P])
        before = sb("before", [P, P], F16)
        ones16 = sb("ones16", [P, P], F16)
        ones_row = sb("ones_row", [1, P])
        ones8 = sb("ones8", [P, E])
        iota_r = sb("iota_r", [P, P], F16)
        iota_s = sb("iota_s", [P, ST], I32)
        token1 = sb("token1", [P, TILES])
        rev = sb("rev", [P, E])
        steps128 = sb("steps128", [P, TILES - 1])
        not_first = sb("not_first", [P, E * TILES])
        neg_half = sb("neg_half", [P, GT])
        zero_row = sb("zero_row", [1, ROW])

        ctx_sb = sb("ctx_sb", [CTX, B, D])
        ctxT = gathered[:, 3072:3380].rearrange("p (k c) -> p k c", k=KD)
        kT = gathered[:, 3380:3688].rearrange("p (k c) -> p k c", k=KD)
        qkT = sb("qkT", [P, KD, B * CTX])
        qbias = sb("qbias", [1, B * CTX])
        bq_sb = sb("bq_sb", [P, KD])
        bk_sb = sb("bk_sb", [P, KD])
        b1_sb = gathered[0:E * FC, 3688:3688 + P]
        wr_sb = sb("wr_sb", [P, KD, E])
        probsT = sb("probsT", [CTX, GT * P])
        stats = sb("stats", [P, GT, 6])
        var_eps = sb("var_eps", [P, GT])
        smax = sb("smax", [P, GT])
        nbias = sb("nbias", [P, GT])
        ssum = sb("ssum", [P, TILES])
        rsum = sb("rsum", [P, TILES])

        lmax = sb("lmax", [P, TPB])
        ldiff = sb("ldiff", [P, TPB, E])
        lexp = sb("lexp", [P, TPB, E])
        lrev = sb("lrev", [P, TPB, E])
        lrmax = sb("lrmax", [P, TPB])
        lsum = sb("lsum", [P, TPB])
        chosen = sb("chosen", [P, E, TILES], F16)
        upto = sb("upto", [P, E * TILES])
        place = sb("place", [P, E * TILES])
        more = sb("more", [P, E, TILES - 1])
        extra = sb("extra", [P, E])
        last = sb("last", [P, E])
        base = sb("base", [P, E])
        pos = sb("pos", [P, TILES], I32)
        pos_row = sb("pos_row", [P, TILES], I32)
        pos_rowf = sb("pos_rowf", [P, TILES])
        pos_slot = sb("pos_slot", [P, TILES], I32)
        slot_eq = gathered[:, 0:TILES * ST].rearrange("p (t s) -> p t s", t=TILES)
        slot_token = gathered[:, 512:512 + TILES * ST // 2].bitcast(F16).rearrange("p (t s) -> p t s", t=TILES)
        done_e = sb("done_e", [1, ST, E])
        slot_ef = sb("slot_ef", [1, ST])
        slot_e = sb("slot_e", [1, ST], I32)
        empty = sb("empty", [P, ST])
        from_row = sb("from_row", [P, ST], I32)
        to_row = sb("to_row", [P, ST], I32)

        free = stage[:, :, :].rearrange("p r n -> p (r n)")
        xs = [free[:, i * D:(i + 1) * D] for i in range(2)]
        out_sb = [free[:, (2 + i) * D:(3 + i) * D] for i in range(2)]
        y_sb = free[:, 4 * D:5 * D]
        x_hi = [free[:, (10 + i) * P:(11 + i) * P].bitcast(F16) for i in range(2)]
        x_lo = [free[:, (12 + i) * P:(13 + i) * P].bitcast(F16) for i in range(2)]

        bank = [stack.enter_context(nc.psum_tensor(f"bank{i}", [P, 512], F32)) for i in range(8)]
        ps_xT = [bank[0], bank[1]]
        ps_att = [bank[2], bank[3]]
        ps_sc = bank[4]
        ps_pT = bank[5]
        ps_logit = bank[6][:, 0:TILES * E].rearrange("p (t e) -> p t e", e=E)
        ps_rank = bank[6][:, 128:256]
        ps_total = bank[6][:, 256:384]
        ps_inv = bank[6][:, 384:384 + ST]
        ps_h = [[bank[0], bank[1]], [bank[2], bank[3]]]
        ps_x = [bank[4][:, 0:D], bank[6][:, 0:D]]
        ps_y = [bank[5][:, 0:D], bank[7][:, 0:D]]

        ctx_in, wk_in, wq_in, small_in, b1_in, b2_in = (sem(n) for n in (
            "ctx_in", "wk_in", "wq_in", "small_in", "b1_in", "b2_in"))
        x_in = [sem(f"x_in{b}") for b in range(B)]
        piece_in = [sem(f"piece_in{r}") for r in range(RING)]
        rows_out = [sem(f"rows_out{b}") for b in range(B)]
        zero_out = sem("zero_out")
        filled, consts = sem("filled"), sem("consts")
        setup_T, setup_TC, setup_k, setup_kC, setup_q, setup_qC = (sem(n) for n in (
            "setup_T", "setup_TC", "setup_k", "setup_kC", "setup_q", "setup_qC"))
        piece_hi, piece_lo = sem("piece_hi"), sem("piece_lo")
        var_ready, rstd_ready, xn_ready, xT_ready, xT_copied = (sem(n) for n in (
            "var_ready", "rstd_ready", "xn_ready", "xT_ready", "xT_copied"))
        score_ready, nbias_ready, exp_ready, pT_ready, pT_copied, att_ready, x1_ready, logit_ready = (
            sem(n) for n in ("score_ready", "nbias_ready", "exp_ready", "pT_ready", "pT_copied",
                             "att_ready", "x1_ready", "logit_ready"))
        ldiff_ready, lexp_ready, rows_ready, chosen_ready, rank_ready = (sem(n) for n in (
            "ldiff_ready", "lexp_ready", "rows_ready", "chosen_ready", "rank_ready"))
        slot_ready, onehot_ready, inv_ready, index_ready, table_ready = (sem(n) for n in (
            "slot_ready", "onehot_ready", "inv_ready", "index_ready", "table_ready"))
        dve_step = sem("dve_step")
        got = [sem(f"got{i}") for i in range(2)]
        stored = [sem(f"stored{i}") for i in range(2)]
        xs_ready, fT_ready, xhi_ready, xlo_ready, mm1_ready, gelu_ready = (sem(n) for n in (
            "xs_ready", "fT_ready", "xhi_ready", "xlo_ready", "mm1_ready", "gelu_ready"))
        hhi_ready, hlo_ready, mm2_ready, y_ready, out_ready = (sem(n) for n in (
            "hhi_ready", "hlo_ready", "mm2_ready", "y_ready", "out_ready"))

        x_v = x.rearrange("b (p j) d -> b p j d", p=P)
        rows_v = scratch[1:TOKENS + 1, :].rearrange("(b p j) r -> b p j r", b=B, p=P)
        out_rows = out.rearrange("b s d -> (b s) d")

        def piece_views(i):
            e, kind = divmod(i, 4)
            if kind < 2:
                src = w1[e, kind * P:(kind + 1) * P, :]
                at = (e * KD + kind) * F
                return src, stage[:, i % RING, :], w1_hi[:, at:at + F], w1_lo[:, at:at + F]
            half = (kind - 2) * (F // 2)
            src = w2[e, half:half + F // 2, :].rearrange("(c p) d -> p c d", p=P)
            at = e * FC * D + (kind - 2) * PIECE
            return (src, stage[:, i % RING, :].rearrange("p (c d) -> p c d", d=D),
                    w2_hi[:, at:at + PIECE], w2_lo[:, at:at + PIECE])

        LN = [("first", 0)]
        for g in range(GROUPS):
            if g + 1 < GROUPS:
                LN.append(("first", g + 1))
            LN.append(("second", g))
        seq_of = {key: n for n, key in enumerate(LN)}

        block = stack.enter_context(nc.Block())

        @block.sync
        def _(sp):
            sp.dma_start(ctx_sb[:, :, :], ctx.rearrange("b c d -> c b d")).then_inc(ctx_in, 16)
            sp.dma_start(wk_sb, wk.rearrange("(k p) d -> p k d", p=P)).then_inc(wk_in, 16)
            sp.dma_start(rows[:, 0:TPB, 0:D], x_v[0]).then_inc(x_in[0], 16)
            sp.dma_start(wq_sb, wq.rearrange("(k p) d -> p k d", p=P)).then_inc(wq_in, 16)
            sp.dma_start(wr_sb[:, :, :], wr.rearrange("(k p) e -> p k e", p=P)).then_inc(small_in, 16)
            with nc.allow_non_contiguous_dma(reason="two bias vectors of 256 elements"):
                sp.dma_start(bk_sb[:, :], bk.rearrange("(k p) -> p k", p=P)).then_inc(small_in, 16)
                sp.dma_start(bq_sb[:, :], bq.rearrange("(k p) -> p k", p=P)).then_inc(small_in, 16)
            sp.dma_start(b1_sb, b1.rearrange("e (c p) -> (e c) p", p=P)).then_inc(b1_in, 16)
            sp.dma_start(rows[:, TPB:TILES, 0:D], x_v[1]).then_inc(x_in[1], 16)

            def load_piece(i):
                if i >= RING:
                    sp.wait_ge(piece_lo, i - RING + 1)
                src, dst, _, _ = piece_views(i)
                sp.dma_start(dst, src).then_inc(piece_in[i % RING], 16)

            def store_rows(b):
                sp.wait_ge(rows_ready, b + 1)
                sp.dma_start(rows_v[b], rows[:, b * TPB:(b + 1) * TPB, :]).then_inc(rows_out[b], 16)

            for i in range(PIECES):
                load_piece(i)
                if i == RING:
                    sp.wait_ge(filled, 1)
                    sp.dma_start(scratch[0:1, :], zero_row[:, :]).then_inc(zero_out, 16)
                    sp.dma_start(b2_rep[:, :], b2.rearrange("e d -> (e d)").partition_broadcast(P)
                                 ).then_inc(b2_in, 16)
                if i == STORE_AT:
                    store_rows(0)
            store_rows(1)

        @block.gpsimd
        def _(pool):
            pool.memset(zero_row[:, :], 0.0)
            pool.memset(ident[:, :], 0.0)
            pool.memset(before[:, :], 1.0)
            pool.memset(not_first[:, :], 1.0)
            pool.memset(ones16[:, :], 1.0)
            pool.memset(ones_row[:, :], 1.0)
            pool.memset(ones8[:, :], 1.0)
            pool.memset(neg_half[:, :], -0.5).then_inc(filled, 1)
            pool.wait_ge(filled, 1)
            pool.affine_select(out=ident[:, :], in_=ident[:, :], pattern=[[-1, P]], compare_op=ALU.not_equal,
                               fill=1.0, base=0, channel_multiplier=1).then_inc(consts, 1)
            pool.affine_select(out=before[:, :], in_=before[:, :], pattern=[[1, P]], compare_op=ALU.is_gt,
                               fill=0.0, base=0, channel_multiplier=-1)
            nf = not_first[:, :].rearrange("p (e t) -> p e t", e=E)
            pool.affine_select(out=nf, in_=nf, pattern=[[0, E], [1, TILES]], compare_op=ALU.is_gt,
                               fill=0.0, base=0, channel_multiplier=0)
            pool.iota(iota_r[:, :], pattern=[[1, P]], base=0, channel_multiplier=0,
                      allow_small_or_imprecise_dtypes=True)
            pool.iota(iota_s[:, :], pattern=[[1, ST]], base=0, channel_multiplier=0)
            pool.iota(token1[:, :].rearrange("p (b j) -> p b j", b=B), pattern=[[S, B], [1, TPB]], base=1,
                      channel_multiplier=TPB, allow_small_or_imprecise_dtypes=True)
            pool.iota(rev[:, :], pattern=[[-1, E]], base=E, channel_multiplier=0,
                      allow_small_or_imprecise_dtypes=True)
            pool.iota(steps128[:, :], pattern=[[P, TILES - 1]], base=P, channel_multiplier=0,
                      allow_small_or_imprecise_dtypes=True).then_inc(consts, 1)

            for n, (_, g) in enumerate(LN):
                pool.wait_ge(var_ready, n + 1)
                pool.tensor_tensor(rows[:, g * GT:(g + 1) * GT, RSTD], var_eps[:, :], neg_half[:, :],
                                   ALU.pow).then_inc(rstd_ready, 1)

            def gather(s):
                pool.indirect_dma_start(
                    out=gathered[:, s * ROW:(s + 1) * ROW], out_offset=None, in_=scratch[:, :],
                    in_offset=bass.IndirectOffsetOnAxis(ap=from_row[:, s:s + 1], axis=0),
                    bounds_check=TOKENS, oob_is_err=False).then_inc(got[s % 2], 16)

            pool.wait_ge(index_ready, 2)
            pool.wait_ge(zero_out, 16)
            for b in range(B):
                pool.wait_ge(rows_out[b], 16)
            gather(0)
            gather(1)
            for s in range(SLOTS):
                if s + 2 < SLOTS:
                    pool.wait_ge(xs_ready, s + 1)
                    gather(s + 2)
                pool.wait_ge(out_ready, s + 1)
                pool.indirect_dma_start(
                    out=out_rows, out_offset=bass.IndirectOffsetOnAxis(ap=to_row[:, s:s + 1], axis=0),
                    in_=out_sb[s % 2], in_offset=None,
                    bounds_check=TOKENS - 1, oob_is_err=False).then_inc(stored[s % 2], 16)
            for q in range(2):
                pool.wait_ge(stored[q], 16 * ((SLOTS - q + 1) // 2))

        @block.scalar
        def _(act):
            act.wait_ge(setup_T, 1)
            nc.scalar.copy(wkT[:, 0, :], bank[0][:, 0:D])
            nc.scalar.copy(wkT[:, 1, :], bank[1][:, 0:D])
            for b in range(B):
                nc.scalar.copy(ctxT[:, :, b * CTX:(b + 1) * CTX],
                               bank[2][:, b * 2 * CTX:(b + 1) * 2 * CTX].rearrange("p (k c) -> p k c", k=KD))
            act.wait_ge(setup_T, 2)
            nc.scalar.copy(b1_T[:, :], bank[3][:, 0:E * FC]).then_inc(setup_TC, 1)
            act.wait_ge(setup_k, 1)
            act.wait_ge(small_in, 48)
            for k in range(KD):
                ins = nc.scalar.activation(kT[:, k, :], bank[5][:, k * B * CTX:(k + 1) * B * CTX], ACT.Identity,
                                           bias=bk_sb[:, k:k + 1])
            ins.then_inc(setup_kC, 1)
            act.wait_ge(setup_q, 1)
            for k in range(KD):
                nc.scalar.copy(qkT[:, k, :], bank[7][:, k * B * CTX:(k + 1) * B * CTX])
            nc.scalar.copy(qbias[:, :], bank[7][0:1, 2 * B * CTX:3 * B * CTX]).then_inc(setup_qC, 1)

            def split_hi(i):
                _, st, hi, _ = piece_views(i)
                act.wait_ge(piece_in[i % RING], 16 * (i // RING + 1))
                nc.scalar.activation(hi, stage[:, i % RING, :], ACT.Copy, scale=WS).then_inc(piece_hi, 1)

            def copy_xT(n):
                act.wait_ge(xT_ready, n + 1)
                if n >= 2:
                    kind, g = LN[n - 2]
                    act.wait_ge(score_ready if kind == "first" else logit_ready, g + 1)
                for k in range(KD):
                    ins = nc.scalar.copy(xnT[n % 2][:, k, :], ps_xT[k][:, :])
                ins.then_inc(xT_copied, 1)

            def exps(g):
                act.wait_ge(nbias_ready, g + 1)
                if g:
                    act.wait_ge(pT_ready, g)
                for j in range(GT):
                    ins = nc.scalar.activation(probs[:, j, 0:CTX], ps_sc[:, j * P:j * P + CTX], ACT.Exp,
                                               bias=nbias[:, j:j + 1], scale=ATT_SCALE,
                                               accum_out=ssum[:, g * GT + j:g * GT + j + 1])
                ins.then_inc(exp_ready, 1)

            def copy_pT(g):
                act.wait_ge(pT_ready, g + 1)
                if g:
                    act.wait_ge(att_ready, g)
                nc.scalar.copy(probsT[:, :], ps_pT[0:CTX, :]).then_inc(pT_copied, 1)

            def logit_exp(b):
                act.wait_ge(ldiff_ready, b + 1)
                nc.scalar.activation(lexp[:, :, :], ldiff[:, :, :], ACT.Exp).then_inc(lexp_ready, 1)

            todo = list(range(PIECES))

            def split(n):
                for _ in range(min(n, len(todo))):
                    split_hi(todo.pop(0))

            split(2)
            copy_xT(seq_of["first", 0])
            exps(0)
            for g in range(GROUPS):
                if g + 1 < GROUPS:
                    copy_xT(seq_of["first", g + 1])
                split(SPLIT_ACT[0])
                copy_pT(g)
                split(SPLIT_ACT[1])
                if g + 1 < GROUPS:
                    exps(g + 1)
                split(SPLIT_ACT[2])
                copy_xT(seq_of["second", g])
                if g % 2:
                    split(2)
                    logit_exp(g // 2)
            split(PIECES)

            def x_high(s, q, reuse):
                act.wait_ge(fT_ready, s + 1)
                if reuse:
                    act.wait_ge(mm1_ready, 2 * s - 2)
                nc.scalar.activation(x_hi[q], ps_x[q], ACT.Copy, scale=XS).then_inc(xhi_ready, 1)

            def gelus(s, q, half, e, reuse):
                act.wait_ge(mm1_ready, 2 * s + half + 1)
                if reuse:
                    act.wait_ge(hlo_ready, 2 * s - 3 + half)
                for c in range(half * 4, half * 4 + 4):
                    ins = nc.scalar.activation(h[q][:, c * P:(c + 1) * P], ps_h[q][half][:, (c % 4) * P:(c % 4 + 1) * P],
                                               ACT.Gelu, bias=b1_T[:, bass.ds(e * FC + c, 1)],
                                               scale=1.0 / (XS * WS))
                ins.then_inc(gelu_ready, 1)

            def step(s, q):
                full = isinstance(s, int)
                e = act.value_load(slot_e[0:1, bass.ds(s + 1, 1)], min_val=0, max_val=E - 1)
                gelus(s + 1, 1 - q, 0, e, not full or s + 1 >= 2)
                if not full or s + 2 < SLOTS:
                    x_high(s + 2, q, True)
                gelus(s + 1, 1 - q, 1, e, not full or s + 1 >= 2)

            act.wait_ge(table_ready, 1)
            x_high(0, 0, False)
            x_high(1, 1, False)
            e0 = act.value_load(slot_e[0:1, 0:1], min_val=0, max_val=E - 1)
            gelus(0, 0, 0, e0, False)
            gelus(0, 0, 1, e0, False)
            step(0, 0)
            step(1, 1)
            with act.Fori(1, LOOP_END) as n:
                step(2 * n, 0)
                step(2 * n + 1, 1)
            for s in range(2 * LOOP_END, SLOTS - 1):
                step(s, s % 2)

        @block.tensor
        def _(pe):
            def mm(o, lhsT, rhs, start, stop):
                return nc.tensor.matmul(o, lhsT, rhs, start=start, stop=stop)

            pe.wait_ge(consts, 1)
            pe.wait_ge(wk_in, 16)
            for k in range(KD):
                for m in range(KD):
                    nc.tensor.transpose(bank[k][:, m * P:(m + 1) * P], wk_sb[:, m, k * P:(k + 1) * P], ident[:, :])
            pe.wait_ge(ctx_in, 16)
            for b in range(B):
                for k in range(KD):
                    at = (b * KD + k) * CTX
                    ins = nc.tensor.transpose(bank[2][:, at:at + CTX], ctx_sb[:, b, k * P:(k + 1) * P],
                                              ident[0:CTX, 0:CTX])
            ins.then_inc(setup_T, 1)
            pe.wait_ge(b1_in, 16)
            nc.tensor.transpose(bank[3][:, 0:E * FC], b1_sb, ident[0:E * FC, 0:E * FC]).then_inc(setup_T, 1)
            pe.wait_ge(setup_TC, 1)
            for m in range(KD):
                for k in range(KD):
                    ins = mm(bank[5][:, m * B * CTX:(m + 1) * B * CTX], wkT[:, k, m * P:(m + 1) * P], ctxT[:, k, :],
                             k == 0, k == KD - 1)
            ins.then_inc(setup_k, 1)

            def transposes(n):
                pe.wait_ge(xn_ready, n + 1)
                if n:
                    pe.wait_ge(xT_copied, n)
                for k in range(KD):
                    for j in range(GT):
                        ins = nc.tensor.transpose(ps_xT[k][:, j * P:(j + 1) * P], xn[n % 2][:, j, k * P:(k + 1) * P],
                                                  ident[:, :])
                ins.then_inc(xT_ready, 1)

            transposes(0)
            pe.wait_ge(setup_kC, 1)
            pe.wait_ge(wq_in, 16)
            for m in range(KD):
                for k in range(KD):
                    mm(bank[7][:, m * B * CTX:(m + 1) * B * CTX], wq_sb[:, k, m * P:(m + 1) * P], kT[:, k, :],
                       k == 0, k == KD - 1)
            for k in range(KD):
                ins = mm(bank[7][0:1, 2 * B * CTX:3 * B * CTX], bq_sb[:, k:k + 1], kT[:, k, :], k == 0, k == KD - 1)
            ins.then_inc(setup_q, 1)

            def scores(g):
                n, b = seq_of["first", g], g * GT // TPB
                pe.wait_ge(xT_copied, n + 1)
                if g:
                    pe.wait_ge(exp_ready, g)
                cols = slice(b * CTX, (b + 1) * CTX)
                for j in range(GT):
                    o = ps_sc[:, j * P:j * P + CTX]
                    for k in range(KD):
                        mm(o, xnT[n % 2][:, k, j * P:(j + 1) * P], qkT[:, k, cols], k == 0, False)
                    ins = mm(o, ones_row[:, :], qbias[:, cols], False, True)
                ins.then_inc(score_ready, 1)

            def probs_T(g):
                pe.wait_ge(exp_ready, g + 1)
                if g:
                    pe.wait_ge(pT_copied, g)
                for j in range(GT):
                    ins = nc.tensor.transpose(ps_pT[0:CTX, j * P:(j + 1) * P], probs[:, j, 0:CTX], ident[:, :])
                ins.then_inc(pT_ready, 1)

            def attend(g):
                b = g * GT // TPB
                pe.wait_ge(pT_copied, g + 1)
                if g:
                    pe.wait_ge(x1_ready, g)
                for j in range(GT):
                    ins = mm(ps_att[j // 2][:, (j % 2) * D:(j % 2 + 1) * D], probsT[:, j * P:(j + 1) * P],
                             ctx_sb[:, b, :], True, True)
                ins.then_inc(att_ready, 1)

            def router(g):
                n = seq_of["second", g]
                pe.wait_ge(xT_copied, n + 1)
                if g * GT % TPB == 0 and g:
                    pe.wait_ge(ldiff_ready, g * GT // TPB)
                for j in range(GT):
                    for k in range(KD):
                        ins = mm(ps_logit[:, g * GT + j, :], xnT[n % 2][:, k, j * P:(j + 1) * P], wr_sb[:, k, :],
                                 k == 0, k == KD - 1)
                ins.then_inc(logit_ready, 1)

            pe.wait_ge(setup_qC, 1)
            pe.wait_ge(small_in, 48)
            scores(0)
            for g in range(GROUPS):
                if g + 1 < GROUPS:
                    transposes(seq_of["first", g + 1])
                probs_T(g)
                attend(g)
                if g + 1 < GROUPS:
                    scores(g + 1)
                transposes(seq_of["second", g])
                router(g)

            pe.wait_ge(chosen_ready, 2)
            pe.wait_ge(consts, 2)
            chosen_all = chosen[:, :, :].rearrange("p e t -> p (e t)")
            mm(ps_rank, before[:, :], chosen_all, True, True)
            mm(ps_total, ones16[:, :], chosen_all, True, True).then_inc(rank_ready, 1)
            pe.wait_ge(slot_ready, 1)
            for t in range(TILES):
                pe.wait_ge(onehot_ready, t + 1)
                ins = mm(ps_inv, row_onehot[:, t, :], slot_token[:, t, :], t == 0, t == TILES - 1)
            ins.then_inc(inv_ready, 1)

            def slot_T(s, q, reuse):
                pe.wait_ge(xs_ready, s + 1)
                if reuse:
                    pe.wait_ge(xlo_ready, s - 1)
                for k in range(KD):
                    ins = nc.tensor.transpose(ps_x[q][:, k * P:(k + 1) * P], xs[q][:, k * P:(k + 1) * P], ident[:, :])
                ins.then_inc(fT_ready, 1)

            def layer1(s, q, reuse):
                e = pe.value_load(slot_e[0:1, bass.ds(s, 1)], min_val=0, max_val=E - 1)
                pe.wait_ge(xlo_ready, s + 1)
                for half in range(2):
                    if reuse:
                        pe.wait_ge(gelu_ready, 2 * s - 3 + half)
                    for c in range(half * 4, half * 4 + 4):
                        o = ps_h[q][half][:, (c % 4) * P:(c % 4 + 1) * P]
                        terms = [(w, v, k) for k in range(KD)
                                 for w, v in ((w1_lo, x_hi[q]), (w1_hi, x_lo[q]), (w1_hi, x_hi[q]))]
                        for n, (w, v, k) in enumerate(terms):
                            ins = mm(o, w[:, bass.ds(e * (KD * F) + (k * F + c * P), P)], v[:, k * P:(k + 1) * P],
                                     n == 0, n == len(terms) - 1)
                    ins.then_inc(mm1_ready, 1)

            def layer2(s, q, reuse):
                e = pe.value_load(slot_e[0:1, bass.ds(s, 1)], min_val=0, max_val=E - 1)
                if reuse:
                    pe.wait_ge(y_ready, s - 1)
                for half in range(2):
                    pe.wait_ge(hlo_ready, 2 * s + half + 1)
                    for c in range(half * 4, half * 4 + 4):
                        for v, w in ((h_lo[q], w2_hi), (h_hi[q], w2_lo), (h_hi[q], w2_hi)):
                            ins = mm(ps_y[q], v[:, c * P:(c + 1) * P], w[:, bass.ds(e * (FC * D) + c * D, D)],
                                     c == 0 and v is h_lo[q], c == FC - 1 and v is h_hi[q] and w is w2_hi)
                ins.then_inc(mm2_ready, 1)

            def step(s, q):
                full = isinstance(s, int)
                if not full or s + 1 < SLOTS:
                    layer1(s + 1, 1 - q, not full or s + 1 >= 2)
                if not full or s + 2 < SLOTS:
                    slot_T(s + 2, q, True)
                layer2(s, q, not full or s >= 2)

            slot_T(0, 0, False)
            slot_T(1, 1, False)
            pe.wait_ge(piece_lo, PIECES)
            layer1(0, 0, False)
            step(0, 0)
            step(1, 1)
            with pe.Fori(1, LOOP_END) as n:
                step(2 * n, 0)
                step(2 * n + 1, 1)
            for s in range(2 * LOOP_END, SLOTS):
                step(s, s % 2)

        @block.vector
        def _(dve):
            steps = [0]

            def link(ins):
                steps[0] += 1
                ins.then_inc(dve_step, 1)
                dve.wait_ge(dve_step, steps[0])

            def split_lo(i):
                _, _, hi, lo = piece_views(i)
                dve.wait_ge(piece_hi, i + 1)
                nc.vector.scalar_tensor_tensor(lo, stage[:, i % RING, :], WS, hi, ALU.mult, ALU.subtract
                                               ).then_inc(piece_lo, 1)

            todo = list(range(PIECES))

            def split(n):
                for _ in range(min(n, len(todo))):
                    split_lo(todo.pop(0))

            def ln_stats(g):
                for j in range(GT):
                    ins = nc.vector.bn_stats(stats[:, j, :], rows[:, g * GT + j, 0:D])
                link(ins)
                for j in range(GT):
                    ins = nc.vector.bn_aggr(rows[:, g * GT + j, MEAN:MEAN + 2], stats[:, j, :])
                link(ins)
                nc.vector.tensor_scalar(var_eps[:, :], rows[:, g * GT:(g + 1) * GT, MEAN + 1], EPS, None, ALU.add
                                        ).then_inc(var_ready, 1)

            def ln_apply(n, g):
                dve.wait_ge(rstd_ready, n + 1)
                if n >= 2:
                    dve.wait_ge(xT_ready, n - 1)
                for j in range(GT):
                    t = g * GT + j
                    ins = nc.vector.tensor_scalar(xn[n % 2][:, j, :], rows[:, t, 0:D], rows[:, t, MEAN:MEAN + 1],
                                                  rows[:, t, RSTD:RSTD + 1], ALU.subtract, ALU.mult)
                ins.then_inc(xn_ready, 1)

            def score_max(g):
                dve.wait_ge(score_ready, g + 1)
                link(nc.vector.reduce_max(smax[:, :], ps_sc[:, :].rearrange("p (j c) -> p j c", j=GT)[:, :, 0:CTX], AXX))
                if g:
                    dve.wait_ge(exp_ready, g)
                nc.vector.tensor_scalar(nbias[:, :], smax[:, :], -ATT_SCALE, None, ALU.mult).then_inc(nbias_ready, 1)

            def add_attention(g):
                dve.wait_ge(exp_ready, g + 1)
                link(nc.vector.reciprocal(rsum[:, g * GT:(g + 1) * GT], ssum[:, g * GT:(g + 1) * GT]))
                dve.wait_ge(att_ready, g + 1)
                for j in range(GT):
                    t = g * GT + j
                    ins = nc.vector.scalar_tensor_tensor(
                        rows[:, t, 0:D], ps_att[j // 2][:, (j % 2) * D:(j % 2 + 1) * D], rsum[:, t:t + 1],
                        rows[:, t, 0:D], ALU.mult, ALU.add)
                steps[0] += 1
                ins.then_inc(x1_ready, 1)
                dve.wait_ge(x1_ready, g + 1)
                steps[0] -= 1

            def route(b):
                tiles = slice(b * TPB, (b + 1) * TPB)
                logits = ps_logit[:, tiles, :]
                dve.wait_ge(logit_ready, (b + 1) * TPB // GT)
                link(nc.vector.reduce_max(lmax[:, :], logits, AXX))
                if b:
                    dve.wait_ge(lexp_ready, b)
                nc.vector.tensor_tensor(ldiff[:, :, :], logits, lmax[:, :].unsqueeze(2).to_broadcast([P, TPB, E]),
                                        ALU.subtract).then_inc(ldiff_ready, 1)
                dve.wait_ge(ldiff_ready, b + 1)
                link(nc.vector.scalar_tensor_tensor(lrev[:, :, :], ldiff[:, :, :], 0.0,
                                                    rev[:, :].unsqueeze(1).to_broadcast([P, TPB, E]),
                                                    ALU.is_equal, ALU.mult))
                link(nc.vector.reduce_max(lrmax[:, :], lrev[:, :, :], AXX))
                nc.vector.tensor_tensor(chosen[:, :, tiles].rearrange("p e t -> p t e"), lrev[:, :, :],
                                        lrmax[:, :].unsqueeze(2).to_broadcast([P, TPB, E]),
                                        ALU.is_equal).then_inc(chosen_ready, 1)
                dve.wait_ge(lexp_ready, b + 1)
                link(nc.vector.reduce_sum(lsum[:, :], lexp[:, :, :], AXX))
                nc.vector.reciprocal(rows[:, tiles, PMAX], lsum[:, :]).then_inc(rows_ready, 1)

            nc.vector.memset(rows[:, :, PMAX:ROW], 0.0)
            dve.wait_ge(consts, 2)
            dve.wait_ge(x_in[0], 16)
            ln_stats(0)
            ln_apply(0, 0)
            split(1)
            for g in range(GROUPS):
                if g + 1 < GROUPS:
                    if (g + 1) * GT == TPB:
                        dve.wait_ge(x_in[1], 16)
                    ln_stats(g + 1)
                if g == 0:
                    split(1)
                    score_max(0)
                if g + 1 < GROUPS:
                    ln_apply(seq_of["first", g + 1], g + 1)
                split(SPLIT_DVE[0])
                add_attention(g)
                ln_stats(g)
                if g + 1 < GROUPS:
                    score_max(g + 1)
                ln_apply(seq_of["second", g], g)
                split(SPLIT_DVE[1])
                if g % 2:
                    route(g // 2)
            split(PIECES)

            dve.wait_ge(rank_ready, 1)
            link(nc.vector.tensor_tensor_scan(upto[:, :], not_first[:, :], ps_total, 0.0, ALU.mult, ALU.add))
            counts = upto[:, :].rearrange("p (e t) -> p e t", e=E)[:, :, TILES - 1:TILES]
            link(nc.vector.tensor_tensor(more[:, :, :], counts.to_broadcast([P, E, TILES - 1]),
                                         steps128[:, :].unsqueeze(1).to_broadcast([P, E, TILES - 1]), ALU.is_gt))
            nc.vector.tensor_tensor(place[:, :], upto[:, :], ps_total, ALU.subtract)
            link(nc.vector.reduce_sum(extra[:, :], more[:, :, :], AXX))
            link(nc.vector.tensor_tensor_scan(last[:, :], ones8[:, :], extra[:, :], 0.0, ALU.add, ALU.add))
            link(nc.vector.tensor_tensor(base[:, :], last[:, :], extra[:, :], ALU.subtract))
            link(nc.vector.tensor_scalar(base[:, :], base[:, :], float(P), -float(P), ALU.mult, ALU.add))
            link(nc.vector.tensor_tensor(place[:, :], place[:, :], ps_rank, ALU.add))
            place3 = place[:, :].rearrange("p (e t) -> p e t", e=E)
            link(nc.vector.tensor_tensor(place3, place3, base[:, :].unsqueeze(2).to_broadcast([P, E, TILES]), ALU.add))
            link(nc.vector.tensor_tensor(place3, place3, chosen[:, :, :], ALU.mult))
            with nc.allow_low_precision(reason="a sum of integers below 2^24, one of them not zero"):
                link(nc.vector.reduce_sum(pos[:, :], place3.rearrange("p e t -> p t e"), AXX))
            nc.vector.tensor_scalar(pos_row[:, :], pos[:, :], P - 1, None, ALU.bitwise_and)
            link(nc.vector.tensor_scalar(pos_slot[:, :], pos[:, :], P.bit_length() - 1, None, ALU.logical_shift_right))
            nc.vector.tensor_copy(pos_rowf[:, :], pos_row[:, :])
            link(nc.vector.tensor_tensor(slot_eq[:, :, :], iota_s[:, :].unsqueeze(1).to_broadcast([P, TILES, ST]),
                                         pos_slot[:, :].unsqueeze(2).to_broadcast([P, TILES, ST]), ALU.is_equal))
            nc.vector.tensor_tensor(slot_token[:, :, :], slot_eq[:, :, :],
                                    token1[:, :].unsqueeze(2).to_broadcast([P, TILES, ST]), ALU.mult
                                    ).then_inc(slot_ready, 1)
            for t in range(TILES):
                nc.vector.tensor_scalar(row_onehot[:, t, :], iota_r[:, :], pos_rowf[:, t:t + 1], None, ALU.is_equal
                                        ).then_inc(onehot_ready, 1)
            link(nc.vector.tensor_tensor(done_e[:, :, :], last[0:1, :].unsqueeze(1).to_broadcast([1, ST, E]),
                                         iota_s[0:1, :].unsqueeze(2).to_broadcast([1, ST, E]), ALU.is_le))
            link(nc.vector.reduce_sum(slot_ef[:, :], done_e[:, :, :], AXX))
            nc.vector.tensor_scalar(slot_e[:, :], slot_ef[:, :], float(E - 1), None, ALU.min).then_inc(table_ready, 1)
            dve.wait_ge(inv_ready, 1)
            nc.vector.tensor_copy(from_row[:, :], ps_inv).then_inc(index_ready, 1)
            link(nc.vector.tensor_scalar(empty[:, :], ps_inv, 0.0, FAR, ALU.is_equal, ALU.mult))
            nc.vector.scalar_tensor_tensor(to_row[:, :], ps_inv, -1.0, empty[:, :], ALU.add, ALU.add
                                           ).then_inc(index_ready, 1)

            def col(s, c, n=1):
                return gathered[:, bass.ds(s * ROW + c, n)]

            def slot_norm(s, q, m, reuse):
                dve.wait_ge(got[q], 16 * (m + 1))
                if reuse:
                    dve.wait_ge(fT_ready, s - 1)
                nc.vector.tensor_scalar(xs[q], col(s, 0, D), col(s, MEAN), col(s, RSTD),
                                        ALU.subtract, ALU.mult).then_inc(xs_ready, 1)

            def x_low(s, q, reuse):
                dve.wait_ge(xhi_ready, s + 1)
                nc.vector.scalar_tensor_tensor(x_lo[q], ps_x[q], XS, x_hi[q], ALU.mult, ALU.subtract
                                               ).then_inc(xlo_ready, 1)

            def h_split(s, q, half, reuse):
                dve.wait_ge(gelu_ready, 2 * s + half + 1)
                if reuse:
                    dve.wait_ge(mm2_ready, s - 1)
                part = slice(half * 512, half * 512 + 512)
                nc.vector.tensor_scalar(h_hi[q][:, part], h[q][:, part], HS, None, ALU.mult).then_inc(hhi_ready, 1)
                dve.wait_ge(hhi_ready, 2 * s + half + 1)
                nc.vector.scalar_tensor_tensor(h_lo[q][:, part], h[q][:, part], HS, h_hi[q][:, part],
                                               ALU.mult, ALU.subtract).then_inc(hlo_ready, 1)

            def finish(s, q, m, reuse):
                e = dve.value_load(slot_e[0:1, bass.ds(s, 1)], min_val=0, max_val=E - 1)
                dve.wait_ge(mm2_ready, s + 1)
                nc.vector.scalar_tensor_tensor(y_sb, ps_y[q], 1.0 / (HS * WS), b2_rep[:, bass.ds(e * D, D)],
                                               ALU.mult, ALU.add).then_inc(y_ready, 1)
                dve.wait_ge(y_ready, s + 1)
                if reuse:
                    dve.wait_ge(stored[q], 16 * m)
                nc.vector.scalar_tensor_tensor(out_sb[q], y_sb, col(s, PMAX), col(s, 0, D),
                                               ALU.mult, ALU.add).then_inc(out_ready, 1)

            def step(s, q, m):
                full = isinstance(s, int)
                if not full or s + 2 < SLOTS:
                    slot_norm(s + 2, q, m + 1, True)
                for half in range(2):
                    h_split(s, q, half, not full or s >= 2)
                if not full or s + 2 < SLOTS:
                    x_low(s + 2, q, True)
                finish(s, q, m, not full or s >= 2)

            dve.wait_ge(b2_in, 16)
            slot_norm(0, 0, 0, False)
            slot_norm(1, 1, 0, False)
            x_low(0, 0, False)
            x_low(1, 1, False)
            step(0, 0, 0)
            step(1, 1, 0)
            with dve.Fori(1, LOOP_END) as n:
                step(2 * n, 0, n)
                step(2 * n + 1, 1, n)
            for s in range(2 * LOOP_END, SLOTS):
                step(s, s % 2, s // 2)


SPLIT_ACT = (3, 3, 2)
SPLIT_DVE = (4, 4)
STORE_AT = 20
LOOP_END = (SLOTS - 2) // 2

_INS = ["x", "ctx_1024", "L0_xattn_Wq", "L0_xattn_bq", "L0_xattn_Wk", "L0_xattn_bk", "L0_ffn_Wr", "L0_ffn_W1",
        "L0_ffn_b1", "L0_ffn_W2", "L0_ffn_b2"]


def kernel(**inputs):
    import numpy as _np
    import concourse.bacc as _bacc
    from concourse import mybir as _mybir
    from concourse.bass_utils import run_bass_kernel_spmd as _run

    nc = _bacc.Bacc("TRN2", target_bir_lowering=False, num_devices=1)
    arrays, args = {}, []
    for name in _INS:
        a = _np.ascontiguousarray(inputs[name])
        arrays[f"in_{name}_dram"] = a
        args.append(nc.dram_tensor(f"in_{name}_dram", a.shape, _mybir.dt.from_np(a.dtype), kind="ExternalInput").ap())
    args.append(nc.dram_tensor("out_0_dram", (B, S, D), F32, kind="ExternalOutput").ap())
    build(nc, *args)
    r = _run(nc, [arrays], core_ids=[0])
    return r.results[0]["out_0_dram"]
```

```python
from contextlib import ExitStack

import concourse.bass as bass
from concourse import mybir

ALU = mybir.AluOpType
ACT = mybir.ActivationFunctionType
AXX = mybir.AxisListType.X
F32 = mybir.dt.float32
F16 = mybir.dt.float16
I32 = mybir.dt.int32

P = 128
D = 256
KD = D // P
B, S = 2, 1024
CTX = 77
E, F = 8, 1024
FC = F // P
TOKENS = B * S
TILES = TOKENS // P
TPB = S // P
GT = 4
GROUPS = TILES // GT
SLOTS = (TOKENS + E * (P - 1)) // P
ST = SLOTS + 1
ROW = D + 4
MEAN, RSTD, PMAX = D, D + 1, D + 2
EPS = 1e-5
ATT_SCALE = 1.0 / 32.0
XS = 64.0
WS = 64.0
HS = 16.0
WE = 2 * KD * F
PIECE = 1024
PIECES = E * 4
RING = 4
FAR = 8192.0


def build(nc, x, ctx, wq, bq, wk, bk, wr, w1, b1, w2, b2, out):
    assert SLOTS >= E and (TOKENS + 1) < FAR
    with ExitStack() as stack:
        def sb(name, shape, dt=F32):
            return stack.enter_context(nc.sbuf_tensor(name, shape, dt))

        def sem(name):
            return stack.enter_context(nc.semaphore(name))

        scratch = nc.dram_tensor("token_rows", [TOKENS + 1, ROW], F32, kind="Internal").ap()

        w1_pair = sb("w1_pair", [P, E * WE], F16)
        w2_pair = sb("w2_pair", [P, E * WE], F16)
        stage = sb("stage", [P, RING, PIECE])
        b2_rep = sb("b2_rep", [P, E * D])
        b1_T = sb("b1_T", [P, E * FC])
        gathered = sb("gathered", [P, SLOTS * ROW])
        xn = [gathered[:, i * 1024:(i + 1) * 1024].rearrange("p (j d) -> p j d", j=GT) for i in range(2)]
        xnT = [gathered[:, (2 + i) * 1024:(3 + i) * 1024].rearrange("p (k n) -> p k n", k=KD) for i in range(2)]
        probs = gathered[:, 4096:4096 + GT * 80].rearrange("p (j c) -> p j c", j=GT)
        wq_sb = gathered[:, 4416:4928].rearrange("p (k d) -> p k d", k=KD)
        wk_sb = gathered[:, 4928:5440].rearrange("p (k d) -> p k d", k=KD)
        row_onehot = gathered[:, 4416:5440].bitcast(F16).rearrange("p (t r) -> p t r", t=TILES)
        wkT = gathered[:, 5440:5952].rearrange("p (k d) -> p k d", k=KD)
        rows = sb("rows", [P, TILES, ROW])
        rows_flat = rows[:, :, :].rearrange("p t r -> p (t r)")
        h = rows_flat[:, 0:F]
        xs = [rows_flat[:, F + i * D:F + (i + 1) * D] for i in range(2)]
        x_hi = [rows_flat[:, F + 2 * D + i * P:F + 2 * D + (i + 1) * P].bitcast(F16) for i in range(2)]
        x_lo = [rows_flat[:, F + 3 * D + i * P:F + 3 * D + (i + 1) * P].bitcast(F16) for i in range(2)]
        h_hi = [rows_flat[:, 2048 + i * 512:2560 + i * 512].bitcast(F16) for i in range(2)]
        h_lo = [rows_flat[:, 3072 + i * 512:3584 + i * 512].bitcast(F16) for i in range(2)]

        ident = sb("ident", [P, P])
        before = sb("before", [P, P], F16)
        ones16 = sb("ones16", [P, P], F16)
        ones_row = sb("ones_row", [1, P])
        ones8 = sb("ones8", [P, E])
        iota_r = sb("iota_r", [P, P], F16)
        iota_s = sb("iota_s", [P, ST], I32)
        token1 = sb("token1", [P, TILES])
        rev = sb("rev", [P, E])
        steps128 = sb("steps128", [P, TILES - 1])
        not_first = sb("not_first", [P, E * TILES])
        neg_half = sb("neg_half", [P, GT])
        zero_row = sb("zero_row", [1, ROW])

        ctx_sb = sb("ctx_sb", [CTX, B, D])
        ctxT = gathered[:, 3072:3380].rearrange("p (k c) -> p k c", k=KD)
        kT = gathered[:, 3380:3688].rearrange("p (k c) -> p k c", k=KD)
        qkT = sb("qkT", [P, KD, B * CTX])
        qbias = sb("qbias", [1, B * CTX])
        bq_sb = sb("bq_sb", [P, KD])
        bk_sb = sb("bk_sb", [P, KD])
        b1_sb = gathered[0:E * FC, 3688:3688 + P]
        wr_sb = sb("wr_sb", [P, KD, E])
        probsT = sb("probsT", [P, GT * P])
        stats = sb("stats", [P, GT, 6])
        var_eps = sb("var_eps", [P, GT])
        smax = sb("smax", [P, GT])
        nbias = sb("nbias", [P, GT])
        ssum = sb("ssum", [P, TILES])
        rsum = sb("rsum", [P, TILES])

        lmax = sb("lmax", [P, TPB])
        ldiff = sb("ldiff", [P, TPB, E])
        lexp = sb("lexp", [P, TPB, E])
        lrev = sb("lrev", [P, TPB, E])
        lrmax = sb("lrmax", [P, TPB])
        lsum = sb("lsum", [P, TPB])
        chosen = sb("chosen", [P, E, TILES], F16)
        upto = sb("upto", [P, E * TILES])
        place = sb("place", [P, E * TILES])
        more = sb("more", [P, E, TILES - 1])
        extra = sb("extra", [P, E])
        last = sb("last", [P, E])
        base = sb("base", [P, E])
        pos = sb("pos", [P, TILES], I32)
        pos_row = sb("pos_row", [P, TILES], I32)
        pos_rowf = sb("pos_rowf", [P, TILES])
        pos_slot = sb("pos_slot", [P, TILES], I32)
        slot_eq = gathered[:, 0:TILES * ST].rearrange("p (t s) -> p t s", t=TILES)
        slot_token = gathered[:, 512:512 + TILES * ST // 2].bitcast(F16).rearrange("p (t s) -> p t s", t=TILES)
        done_e = sb("done_e", [1, ST, E])
        slot_ef = sb("slot_ef", [1, ST])
        slot_w = sb("slot_w", [1, ST], I32)
        slot_b1 = sb("slot_b1", [1, ST], I32)
        slot_b2 = sb("slot_b2", [1, ST], I32)
        empty = sb("empty", [P, ST])
        from_row = sb("from_row", [P, ST], I32)
        to_row = sb("to_row", [P, ST], I32)

        out_sb = [probsT[:, i * D:(i + 1) * D] for i in range(2)]
        y_sb = sb("y_sb", [P, D])

        bank = [stack.enter_context(nc.psum_tensor(f"bank{i}", [P, 512], F32)) for i in range(8)]
        ps_xT = [bank[0], bank[1]]
        ps_att = [bank[2], bank[3]]
        ps_sc = bank[4]
        ps_pT = bank[5]
        ps_logit = bank[6][:, 0:TILES * E].rearrange("p (t e) -> p t e", e=E)
        ps_rank = bank[6][:, 128:256]
        ps_total = bank[6][:, 256:384]
        ps_inv = bank[6][:, 384:384 + ST]
        ps_h = [[bank[0], bank[1]], [bank[2], bank[3]]]
        ps_x = [bank[4][:, 0:D], bank[6][:, 0:D]]
        ps_y = [bank[5], bank[7]]

        ctx_in, wk_in, wq_in, small_in, b1_in, b2_in = (sem(n) for n in (
            "ctx_in", "wk_in", "wq_in", "small_in", "b1_in", "b2_in"))
        x_in = [sem(f"x_in{b}") for b in range(B)]
        piece_in = [sem(f"piece_in{r}") for r in range(RING)]
        rows_out = [sem(f"rows_out{b}") for b in range(B)]
        zero_out = sem("zero_out")
        filled, consts = sem("filled"), sem("consts")
        setup_T, setup_TC, setup_k, setup_kC, setup_q, setup_qC = (sem(n) for n in (
            "setup_T", "setup_TC", "setup_k", "setup_kC", "setup_q", "setup_qC"))
        piece_hi, piece_lo = sem("piece_hi"), sem("piece_lo")
        var_ready, rstd_ready, xn_ready, xT_ready, xT_copied = (sem(n) for n in (
            "var_ready", "rstd_ready", "xn_ready", "xT_ready", "xT_copied"))
        score_ready, nbias_ready, exp_ready, pT_ready, pT_copied, att_ready, x1_ready, logit_ready = (
            sem(n) for n in ("score_ready", "nbias_ready", "exp_ready", "pT_ready", "pT_copied",
                             "att_ready", "x1_ready", "logit_ready"))
        ldiff_ready, lexp_ready, rows_ready, chosen_ready, rank_ready = (sem(n) for n in (
            "ldiff_ready", "lexp_ready", "rows_ready", "chosen_ready", "rank_ready"))
        slot_ready, onehot_ready, inv_ready, index_ready, table_ready = (sem(n) for n in (
            "slot_ready", "onehot_ready", "inv_ready", "index_ready", "table_ready"))
        dve_step = sem("dve_step")
        got = [sem(f"got{i}") for i in range(AHEAD)]
        landed = sem("landed")
        stored = [sem(f"stored{i}") for i in range(2)]
        xs_ready, fT_ready, xhi_ready, xlo_ready, mm1_ready, gelu_ready = (sem(n) for n in (
            "xs_ready", "fT_ready", "xhi_ready", "xlo_ready", "mm1_ready", "gelu_ready"))
        hhi_ready, hlo_ready, mm2_ready, y_ready, out_ready = (sem(n) for n in (
            "hhi_ready", "hlo_ready", "mm2_ready", "y_ready", "out_ready"))
        y_half = sem("y_half")

        x_v = x.rearrange("b (p j) d -> b p j d", p=P)
        rows_v = scratch[1:TOKENS + 1, :].rearrange("(b p j) r -> b p j r", b=B, p=P)
        out_rows = out.rearrange("b s d -> (b s) d")

        def piece_views(i):
            e, kind = divmod(i, 4)
            if kind < 2:
                src = w1[e, kind * P:(kind + 1) * P, :]
                at = e * WE + kind * F
                return src, stage[:, i % RING, :], w1_pair[:, at:at + F], w1_pair[:, at + KD * F:at + (KD + 1) * F]
            half = (kind - 2) * (F // 2)
            src = w2[e, half:half + F // 2, :].rearrange("(c p) d -> p c d", p=P)
            at = e * WE + (kind - 2) * 2 * PIECE
            pair = w2_pair[:, at:at + 2 * PIECE].rearrange("p (c t d) -> p c t d", t=2, d=D)
            return src, stage[:, i % RING, :].rearrange("p (c d) -> p c d", d=D), pair[:, :, 0, :], pair[:, :, 1, :]

        LN = [("first", 0)]
        for g in range(GROUPS):
            if g + 1 < GROUPS:
                LN.append(("first", g + 1))
            LN.append(("second", g))
        seq_of = {key: n for n, key in enumerate(LN)}

        block = stack.enter_context(nc.Block())

        def slot_offsets(table, engine, width):
            _, values = nc.values_load_multi_w_load_instructions(
                table[0:1, 0:SLOTS], engines=[engine], min_val=0, max_val=(E - 1) * width,
                skip_runtime_bounds_check_because="the table is clamped to the last expert where it is written")
            return values

        @block.sync
        def _(sp):
            sp.dma_start(ctx_sb[:, :, :], ctx.rearrange("b c d -> c b d")).then_inc(ctx_in, 16)
            sp.dma_start(wk_sb, wk.rearrange("(k p) d -> p k d", p=P)).then_inc(wk_in, 16)
            sp.dma_start(rows[:, 0:TPB, 0:D], x_v[0]).then_inc(x_in[0], 16)
            sp.dma_start(wq_sb, wq.rearrange("(k p) d -> p k d", p=P)).then_inc(wq_in, 16)
            sp.dma_start(wr_sb[:, :, :], wr.rearrange("(k p) e -> p k e", p=P)).then_inc(small_in, 16)
            with nc.allow_non_contiguous_dma(reason="two bias vectors of 256 elements"):
                sp.dma_start(bk_sb[:, :], bk.rearrange("(k p) -> p k", p=P)).then_inc(small_in, 16)
                sp.dma_start(bq_sb[:, :], bq.rearrange("(k p) -> p k", p=P)).then_inc(small_in, 16)
            sp.dma_start(b1_sb, b1.rearrange("e (c p) -> (e c) p", p=P)).then_inc(b1_in, 16)
            sp.dma_start(rows[:, TPB:TILES, 0:D], x_v[1]).then_inc(x_in[1], 16)

            def load_piece(i):
                if i >= RING:
                    sp.wait_ge(piece_lo, i - RING + 1)
                src, dst, _, _ = piece_views(i)
                sp.dma_start(dst, src).then_inc(piece_in[i % RING], 16)

            def store_rows(b):
                sp.wait_ge(rows_ready, b + 1)
                sp.dma_start(rows_v[b], rows[:, b * TPB:(b + 1) * TPB, :]).then_inc(rows_out[b], 16)

            for i in range(PIECES):
                load_piece(i)
                if i == RING:
                    sp.wait_ge(filled, 1)
                    sp.dma_start(scratch[0:1, :], zero_row[:, :]).then_inc(zero_out, 16)
                    sp.dma_start(b2_rep[:, :], b2.rearrange("e d -> (e d)").partition_broadcast(P)
                                 ).then_inc(b2_in, 16)
                if i == STORE_AT:
                    store_rows(0)
            store_rows(1)
            for s in range(SLOTS):
                sp.wait_ge(got[s % AHEAD], 16 * (s // AHEAD + 1))
                sp.sem_inc(landed, 1)

        @block.gpsimd
        def _(pool):
            pool.memset(zero_row[:, :], 0.0)
            pool.memset(ident[:, :], 0.0)
            pool.memset(before[:, :], 1.0)
            pool.memset(not_first[:, :], 1.0)
            pool.memset(ones16[:, :], 1.0)
            pool.memset(ones_row[:, :], 1.0)
            pool.memset(ones8[:, :], 1.0)
            pool.memset(neg_half[:, :], -0.5).then_inc(filled, 1)
            pool.wait_ge(filled, 1)
            pool.affine_select(out=ident[:, :], in_=ident[:, :], pattern=[[-1, P]], compare_op=ALU.not_equal,
                               fill=1.0, base=0, channel_multiplier=1).then_inc(consts, 1)
            pool.affine_select(out=before[:, :], in_=before[:, :], pattern=[[1, P]], compare_op=ALU.is_gt,
                               fill=0.0, base=0, channel_multiplier=-1)
            nf = not_first[:, :].rearrange("p (e t) -> p e t", e=E)
            pool.affine_select(out=nf, in_=nf, pattern=[[0, E], [1, TILES]], compare_op=ALU.is_gt,
                               fill=0.0, base=0, channel_multiplier=0)
            pool.iota(iota_r[:, :], pattern=[[1, P]], base=0, channel_multiplier=0,
                      allow_small_or_imprecise_dtypes=True)
            pool.iota(iota_s[:, :], pattern=[[1, ST]], base=0, channel_multiplier=0)
            pool.iota(token1[:, :].rearrange("p (b j) -> p b j", b=B), pattern=[[S, B], [1, TPB]], base=1,
                      channel_multiplier=TPB, allow_small_or_imprecise_dtypes=True)
            pool.iota(rev[:, :], pattern=[[-1, E]], base=E, channel_multiplier=0,
                      allow_small_or_imprecise_dtypes=True)
            pool.iota(steps128[:, :], pattern=[[P, TILES - 1]], base=P, channel_multiplier=0,
                      allow_small_or_imprecise_dtypes=True).then_inc(consts, 1)

            for n, (_, g) in enumerate(LN):
                pool.wait_ge(var_ready, n + 1)
                pool.tensor_tensor(rows[:, g * GT:(g + 1) * GT, RSTD], var_eps[:, :], neg_half[:, :],
                                   ALU.pow).then_inc(rstd_ready, 1)

            def gather(s):
                pool.indirect_dma_start(
                    out=gathered[:, s * ROW:(s + 1) * ROW], out_offset=None, in_=scratch[:, :],
                    in_offset=bass.IndirectOffsetOnAxis(ap=from_row[:, s:s + 1], axis=0),
                    bounds_check=TOKENS, oob_is_err=False).then_inc(got[s % AHEAD], 16)

            pool.wait_ge(index_ready, 2)
            pool.wait_ge(zero_out, 16)
            for b in range(B):
                pool.wait_ge(rows_out[b], 16)
            for s in range(AHEAD):
                gather(s)
            for s in range(SLOTS):
                if s + AHEAD < SLOTS:
                    pool.wait_ge(got[s % AHEAD], 16 * (s // AHEAD + 1))
                    gather(s + AHEAD)
                pool.wait_ge(out_ready, s + 1)
                pool.indirect_dma_start(
                    out=out_rows, out_offset=bass.IndirectOffsetOnAxis(ap=to_row[:, s:s + 1], axis=0),
                    in_=out_sb[s % 2], in_offset=None,
                    bounds_check=TOKENS - 1, oob_is_err=False).then_inc(stored[s % 2], 16)
            for q in range(2):
                pool.wait_ge(stored[q], 16 * ((SLOTS - q + 1) // 2))

        @block.scalar
        def _(act):
            act.wait_ge(setup_T, 1)
            nc.scalar.copy(wkT[:, 0, :], bank[0][:, 0:D])
            nc.scalar.copy(wkT[:, 1, :], bank[1][:, 0:D])
            for b in range(B):
                nc.scalar.copy(ctxT[:, :, b * CTX:(b + 1) * CTX],
                               bank[2][:, b * 2 * CTX:(b + 1) * 2 * CTX].rearrange("p (k c) -> p k c", k=KD))
            act.wait_ge(setup_T, 2)
            nc.scalar.copy(b1_T[:, :], bank[3][:, 0:E * FC]).then_inc(setup_TC, 1)
            act.wait_ge(setup_k, 1)
            act.wait_ge(small_in, 48)
            for k in range(KD):
                ins = nc.scalar.activation(kT[:, k, :], bank[5][:, k * B * CTX:(k + 1) * B * CTX], ACT.Identity,
                                           bias=bk_sb[:, k:k + 1])
            ins.then_inc(setup_kC, 1)
            act.wait_ge(setup_q, 1)
            for k in range(KD):
                nc.scalar.copy(qkT[:, k, :], bank[7][:, k * B * CTX:(k + 1) * B * CTX])
            nc.scalar.copy(qbias[:, :], bank[7][0:1, 2 * B * CTX:3 * B * CTX]).then_inc(setup_qC, 1)

            def split_hi(i):
                _, st, hi, _ = piece_views(i)
                act.wait_ge(piece_in[i % RING], 16 * (i // RING + 1))
                nc.scalar.activation(hi, st, ACT.Copy, scale=WS).then_inc(piece_hi, 1)

            def copy_xT(n):
                act.wait_ge(xT_ready, n + 1)
                if n >= 2:
                    kind, g = LN[n - 2]
                    act.wait_ge(score_ready if kind == "first" else logit_ready, g + 1)
                for k in range(KD):
                    ins = nc.scalar.copy(xnT[n % 2][:, k, :], ps_xT[k][:, :])
                ins.then_inc(xT_copied, 1)

            def exps(g):
                act.wait_ge(nbias_ready, g + 1)
                if g:
                    act.wait_ge(pT_ready, g)
                for j in range(GT):
                    ins = nc.scalar.activation(probs[:, j, 0:CTX], ps_sc[:, j * P:j * P + CTX], ACT.Exp,
                                               bias=nbias[:, j:j + 1], scale=ATT_SCALE,
                                               accum_out=ssum[:, g * GT + j:g * GT + j + 1])
                ins.then_inc(exp_ready, 1)

            def copy_pT(g):
                act.wait_ge(pT_ready, g + 1)
                if g:
                    act.wait_ge(att_ready, g)
                nc.scalar.copy(probsT[0:CTX, :], ps_pT[0:CTX, :]).then_inc(pT_copied, 1)

            def logit_exp(b):
                act.wait_ge(ldiff_ready, b + 1)
                nc.scalar.activation(lexp[:, :, :], ldiff[:, :, :], ACT.Exp).then_inc(lexp_ready, 1)

            todo = list(range(PIECES))

            def split(n):
                for _ in range(min(n, len(todo))):
                    split_hi(todo.pop(0))

            split(2)
            copy_xT(seq_of["first", 0])
            exps(0)
            for g in range(GROUPS):
                if g + 1 < GROUPS:
                    copy_xT(seq_of["first", g + 1])
                split(SPLIT_ACT[0])
                copy_pT(g)
                split(SPLIT_ACT[1])
                if g + 1 < GROUPS:
                    exps(g + 1)
                split(SPLIT_ACT[2])
                copy_xT(seq_of["second", g])
                if g % 2:
                    split(2)
                    logit_exp(g // 2)
            split(PIECES)

            def x_high(s):
                q = s % 2
                act.wait_ge(fT_ready, s + 1)
                if s >= 2:
                    act.wait_ge(mm1_ready, 2 * s - 2)
                nc.scalar.activation(x_hi[q], ps_x[q], ACT.Copy, scale=XS).then_inc(xhi_ready, 1)

            def gelus(s, half):
                q = s % 2
                act.wait_ge(mm1_ready, 2 * s + half + 1)
                if s >= 1:
                    act.wait_ge(hlo_ready, 2 * s - 1 + half)
                for c in range(half * 4, half * 4 + 4):
                    ins = nc.scalar.activation(h[:, c * P:(c + 1) * P], ps_h[q][half][:, (c % 4) * P:(c % 4 + 1) * P],
                                               ACT.Gelu, bias=b1_T[:, bass.ds(b1_at[s] + c, 1)],
                                               scale=1.0 / (XS * WS))
                ins.then_inc(gelu_ready, 1)

            act.wait_ge(table_ready, 1)
            b1_at = slot_offsets(slot_b1, mybir.EngineType.Activation, FC)
            x_high(0)
            x_high(1)
            gelus(0, 0)
            for s in range(SLOTS):
                gelus(s, 1)
                if s + 2 < SLOTS:
                    x_high(s + 2)
                if s + 1 < SLOTS:
                    gelus(s + 1, 0)

        @block.tensor
        def _(pe):
            def mm(o, lhsT, rhs, start, stop):
                return nc.tensor.matmul(o, lhsT, rhs, start=start, stop=stop)

            pe.wait_ge(consts, 1)
            pe.wait_ge(wk_in, 16)
            for k in range(KD):
                for m in range(KD):
                    nc.tensor.transpose(bank[k][:, m * P:(m + 1) * P], wk_sb[:, m, k * P:(k + 1) * P], ident[:, :])
            pe.wait_ge(ctx_in, 16)
            for b in range(B):
                for k in range(KD):
                    at = (b * KD + k) * CTX
                    ins = nc.tensor.transpose(bank[2][:, at:at + CTX], ctx_sb[:, b, k * P:(k + 1) * P],
                                              ident[0:CTX, 0:CTX])
            ins.then_inc(setup_T, 1)
            pe.wait_ge(b1_in, 16)
            nc.tensor.transpose(bank[3][:, 0:E * FC], b1_sb, ident[0:E * FC, 0:E * FC]).then_inc(setup_T, 1)
            pe.wait_ge(setup_TC, 1)
            for m in range(KD):
                for k in range(KD):
                    ins = mm(bank[5][:, m * B * CTX:(m + 1) * B * CTX], wkT[:, k, m * P:(m + 1) * P], ctxT[:, k, :],
                             k == 0, k == KD - 1)
            ins.then_inc(setup_k, 1)

            def transposes(n):
                pe.wait_ge(xn_ready, n + 1)
                if n:
                    pe.wait_ge(xT_copied, n)
                for k in range(KD):
                    for j in range(GT):
                        ins = nc.tensor.transpose(ps_xT[k][:, j * P:(j + 1) * P], xn[n % 2][:, j, k * P:(k + 1) * P],
                                                  ident[:, :])
                ins.then_inc(xT_ready, 1)

            transposes(0)
            pe.wait_ge(setup_kC, 1)
            pe.wait_ge(wq_in, 16)
            for m in range(KD):
                for k in range(KD):
                    mm(bank[7][:, m * B * CTX:(m + 1) * B * CTX], wq_sb[:, k, m * P:(m + 1) * P], kT[:, k, :],
                       k == 0, k == KD - 1)
            for k in range(KD):
                ins = mm(bank[7][0:1, 2 * B * CTX:3 * B * CTX], bq_sb[:, k:k + 1], kT[:, k, :], k == 0, k == KD - 1)
            ins.then_inc(setup_q, 1)

            def scores(g):
                n, b = seq_of["first", g], g * GT // TPB
                pe.wait_ge(xT_copied, n + 1)
                if g:
                    pe.wait_ge(exp_ready, g)
                cols = slice(b * CTX, (b + 1) * CTX)
                for j in range(GT):
                    o = ps_sc[:, j * P:j * P + CTX]
                    for k in range(KD):
                        mm(o, xnT[n % 2][:, k, j * P:(j + 1) * P], qkT[:, k, cols], k == 0, False)
                    ins = mm(o, ones_row[:, :], qbias[:, cols], False, True)
                ins.then_inc(score_ready, 1)

            def probs_T(g):
                pe.wait_ge(exp_ready, g + 1)
                if g:
                    pe.wait_ge(pT_copied, g)
                for j in range(GT):
                    ins = nc.tensor.transpose(ps_pT[0:CTX, j * P:(j + 1) * P], probs[:, j, 0:CTX], ident[:, :])
                ins.then_inc(pT_ready, 1)

            def attend(g):
                b = g * GT // TPB
                pe.wait_ge(pT_copied, g + 1)
                if g:
                    pe.wait_ge(x1_ready, g)
                for j in range(GT):
                    ins = mm(ps_att[j // 2][:, (j % 2) * D:(j % 2 + 1) * D], probsT[0:CTX, j * P:(j + 1) * P],
                             ctx_sb[:, b, :], True, True)
                ins.then_inc(att_ready, 1)

            def router(g):
                n = seq_of["second", g]
                pe.wait_ge(xT_copied, n + 1)
                if g * GT % TPB == 0 and g:
                    pe.wait_ge(ldiff_ready, g * GT // TPB)
                for j in range(GT):
                    for k in range(KD):
                        ins = mm(ps_logit[:, g * GT + j, :], xnT[n % 2][:, k, j * P:(j + 1) * P], wr_sb[:, k, :],
                                 k == 0, k == KD - 1)
                ins.then_inc(logit_ready, 1)

            pe.wait_ge(setup_qC, 1)
            pe.wait_ge(small_in, 48)
            scores(0)
            for g in range(GROUPS):
                if g + 1 < GROUPS:
                    transposes(seq_of["first", g + 1])
                probs_T(g)
                attend(g)
                if g + 1 < GROUPS:
                    scores(g + 1)
                transposes(seq_of["second", g])
                router(g)

            pe.wait_ge(chosen_ready, 2)
            pe.wait_ge(consts, 2)
            chosen_all = chosen[:, :, :].rearrange("p e t -> p (e t)")
            mm(ps_rank, before[:, :], chosen_all, True, True)
            mm(ps_total, ones16[:, :], chosen_all, True, True).then_inc(rank_ready, 1)
            pe.wait_ge(slot_ready, 1)
            for t in range(TILES):
                pe.wait_ge(onehot_ready, t + 1)
                ins = mm(ps_inv, row_onehot[:, t, :], slot_token[:, t, :], t == 0, t == TILES - 1)
            ins.then_inc(inv_ready, 1)

            def slot_T(s):
                q = s % 2
                pe.wait_ge(xs_ready, s + 1)
                if s >= 2:
                    pe.wait_ge(xlo_ready, s - 1)
                for k in range(KD):
                    ins = nc.tensor.transpose(ps_x[q][:, k * P:(k + 1) * P], xs[q][:, k * P:(k + 1) * P], ident[:, :])
                ins.then_inc(fT_ready, 1)

            def w1_at(at, lo, k, c):
                return w1_pair[:, bass.ds(at + (lo * KD * F + k * F + c * P), P)]

            def w2_at(at, c, n):
                return w2_pair[:, bass.ds(at + c * 2 * D, n * D)]

            def addresses(after, this, c):
                if after is not None:
                    for k in range(KD):
                        for lo in range(2):
                            pe.lower_ap(w1_at(after, lo, k, c), for_matmul_weights=True)
                if this is not None:
                    pe.lower_ap(w2_at(this, c - 1, 2))

            def layer1(s, c):
                q = s % 2
                if c == 0:
                    pe.wait_ge(xlo_ready, s + 1)
                if c % 4 == 0 and s >= 2:
                    pe.wait_ge(gelu_ready, 2 * s - 3 + c // 4)
                o = ps_h[q][c // 4][:, (c % 4) * P:(c % 4 + 1) * P]
                terms = [(lo, v, k) for k in range(KD) for lo, v in ((1, x_hi[q]), (0, x_lo[q]), (0, x_hi[q]))]
                for n, (lo, v, k) in enumerate(terms):
                    ins = mm(o, w1_at(w_at[s], lo, k, c), v[:, k * P:(k + 1) * P], n == 0, n == len(terms) - 1)
                if c % 4 == 3:
                    ins.then_inc(mm1_ready, 1)

            def layer2(s, c):
                q, hc = s % 2, slice(c * P, (c + 1) * P)
                if c == 0 and s >= 2:
                    pe.wait_ge(y_ready, s - 1)
                if c % 4 == 0:
                    pe.wait_ge(hlo_ready, 2 * s + c // 4 + 1)
                both = [lambda: mm(ps_y[q][:, :], h_hi[q][:, hc], w2_at(w_at[s], c, 2), c == 0, c == FC - 1),
                        lambda: mm(ps_y[q][:, 0:D], h_lo[q][:, hc], w2_at(w_at[s], c, 1), False, False)]
                for product in (both if c == 0 else both[::-1]):
                    ins = product()
                if c == FC - 1:
                    ins.then_inc(mm2_ready, 1)

            pe.wait_ge(table_ready, 1)
            w_at = slot_offsets(slot_w, mybir.EngineType.PE, WE)
            slot_T(0)
            slot_T(1)
            pe.wait_ge(piece_lo, PIECES)
            for c in range(FC):
                addresses(w_at[0], None, c)
                layer1(0, c)
            for s in range(SLOTS):
                for c in range(FC + 1):
                    one = s + 1 < SLOTS and c < FC
                    addresses(w_at[s + 1] if one else None, w_at[s] if c else None, c)
                    if one:
                        layer1(s + 1, c)
                    if c == 1 and s + 2 < SLOTS:
                        slot_T(s + 2)
                    if c:
                        layer2(s, c - 1)

        @block.vector
        def _(dve):
            steps = [0]

            def link(ins):
                steps[0] += 1
                ins.then_inc(dve_step, 1)
                dve.wait_ge(dve_step, steps[0])

            def split_lo(i):
                _, st, hi, lo = piece_views(i)
                dve.wait_ge(piece_hi, i + 1)
                nc.vector.scalar_tensor_tensor(lo, st, WS, hi, ALU.mult, ALU.subtract
                                               ).then_inc(piece_lo, 1)

            todo = list(range(PIECES))

            def split(n):
                for _ in range(min(n, len(todo))):
                    split_lo(todo.pop(0))

            def ln_stats(g):
                for j in range(GT):
                    ins = nc.vector.bn_stats(stats[:, j, :], rows[:, g * GT + j, 0:D])
                link(ins)
                for j in range(GT):
                    ins = nc.vector.bn_aggr(rows[:, g * GT + j, MEAN:MEAN + 2], stats[:, j, :])
                link(ins)
                nc.vector.tensor_scalar(var_eps[:, :], rows[:, g * GT:(g + 1) * GT, MEAN + 1], EPS, None, ALU.add
                                        ).then_inc(var_ready, 1)

            def ln_apply(n, g):
                dve.wait_ge(rstd_ready, n + 1)
                if n >= 2:
                    dve.wait_ge(xT_ready, n - 1)
                for j in range(GT):
                    t = g * GT + j
                    ins = nc.vector.tensor_scalar(xn[n % 2][:, j, :], rows[:, t, 0:D], rows[:, t, MEAN:MEAN + 1],
                                                  rows[:, t, RSTD:RSTD + 1], ALU.subtract, ALU.mult)
                ins.then_inc(xn_ready, 1)

            def score_max(g):
                dve.wait_ge(score_ready, g + 1)
                link(nc.vector.reduce_max(smax[:, :], ps_sc[:, :].rearrange("p (j c) -> p j c", j=GT)[:, :, 0:CTX], AXX))
                if g:
                    dve.wait_ge(exp_ready, g)
                nc.vector.tensor_scalar(nbias[:, :], smax[:, :], -ATT_SCALE, None, ALU.mult).then_inc(nbias_ready, 1)

            def add_attention(g):
                dve.wait_ge(exp_ready, g + 1)
                link(nc.vector.reciprocal(rsum[:, g * GT:(g + 1) * GT], ssum[:, g * GT:(g + 1) * GT]))
                dve.wait_ge(att_ready, g + 1)
                for j in range(GT):
                    t = g * GT + j
                    ins = nc.vector.scalar_tensor_tensor(
                        rows[:, t, 0:D], ps_att[j // 2][:, (j % 2) * D:(j % 2 + 1) * D], rsum[:, t:t + 1],
                        rows[:, t, 0:D], ALU.mult, ALU.add)
                steps[0] += 1
                ins.then_inc(x1_ready, 1)
                dve.wait_ge(x1_ready, g + 1)
                steps[0] -= 1

            def route(b):
                tiles = slice(b * TPB, (b + 1) * TPB)
                logits = ps_logit[:, tiles, :]
                dve.wait_ge(logit_ready, (b + 1) * TPB // GT)
                link(nc.vector.reduce_max(lmax[:, :], logits, AXX))
                if b:
                    dve.wait_ge(lexp_ready, b)
                nc.vector.tensor_tensor(ldiff[:, :, :], logits, lmax[:, :].unsqueeze(2).to_broadcast([P, TPB, E]),
                                        ALU.subtract).then_inc(ldiff_ready, 1)
                dve.wait_ge(ldiff_ready, b + 1)
                link(nc.vector.scalar_tensor_tensor(lrev[:, :, :], ldiff[:, :, :], 0.0,
                                                    rev[:, :].unsqueeze(1).to_broadcast([P, TPB, E]),
                                                    ALU.is_equal, ALU.mult))
                link(nc.vector.reduce_max(lrmax[:, :], lrev[:, :, :], AXX))
                nc.vector.tensor_tensor(chosen[:, :, tiles].rearrange("p e t -> p t e"), lrev[:, :, :],
                                        lrmax[:, :].unsqueeze(2).to_broadcast([P, TPB, E]),
                                        ALU.is_equal).then_inc(chosen_ready, 1)
                dve.wait_ge(lexp_ready, b + 1)
                link(nc.vector.reduce_sum(lsum[:, :], lexp[:, :, :], AXX))
                nc.vector.reciprocal(rows[:, tiles, PMAX], lsum[:, :]).then_inc(rows_ready, 1)

            nc.vector.memset(rows[:, :, PMAX:ROW], 0.0)
            dve.wait_ge(consts, 2)
            dve.wait_ge(x_in[0], 16)
            ln_stats(0)
            ln_apply(0, 0)
            split(1)
            for g in range(GROUPS):
                if g + 1 < GROUPS:
                    if (g + 1) * GT == TPB:
                        dve.wait_ge(x_in[1], 16)
                    ln_stats(g + 1)
                if g == 0:
                    split(1)
                    score_max(0)
                if g + 1 < GROUPS:
                    ln_apply(seq_of["first", g + 1], g + 1)
                split(SPLIT_DVE[0])
                add_attention(g)
                ln_stats(g)
                if g + 1 < GROUPS:
                    score_max(g + 1)
                ln_apply(seq_of["second", g], g)
                split(SPLIT_DVE[1])
                if g % 2:
                    route(g // 2)
            split(PIECES)

            dve.wait_ge(rank_ready, 1)
            link(nc.vector.tensor_tensor_scan(upto[:, :], not_first[:, :], ps_total, 0.0, ALU.mult, ALU.add))
            counts = upto[:, :].rearrange("p (e t) -> p e t", e=E)[:, :, TILES - 1:TILES]
            link(nc.vector.tensor_tensor(more[:, :, :], counts.to_broadcast([P, E, TILES - 1]),
                                         steps128[:, :].unsqueeze(1).to_broadcast([P, E, TILES - 1]), ALU.is_gt))
            nc.vector.tensor_tensor(place[:, :], upto[:, :], ps_total, ALU.subtract)
            link(nc.vector.reduce_sum(extra[:, :], more[:, :, :], AXX))
            link(nc.vector.tensor_tensor_scan(last[:, :], ones8[:, :], extra[:, :], 0.0, ALU.add, ALU.add))
            link(nc.vector.tensor_tensor(base[:, :], last[:, :], extra[:, :], ALU.subtract))
            link(nc.vector.tensor_scalar(base[:, :], base[:, :], float(P), -float(P), ALU.mult, ALU.add))
            link(nc.vector.tensor_tensor(place[:, :], place[:, :], ps_rank, ALU.add))
            place3 = place[:, :].rearrange("p (e t) -> p e t", e=E)
            link(nc.vector.tensor_tensor(place3, place3, base[:, :].unsqueeze(2).to_broadcast([P, E, TILES]), ALU.add))
            link(nc.vector.tensor_tensor(place3, place3, chosen[:, :, :], ALU.mult))
            with nc.allow_low_precision(reason="a sum of integers below 2^24, one of them not zero"):
                link(nc.vector.reduce_sum(pos[:, :], place3.rearrange("p e t -> p t e"), AXX))
            nc.vector.tensor_scalar(pos_row[:, :], pos[:, :], P - 1, None, ALU.bitwise_and)
            link(nc.vector.tensor_scalar(pos_slot[:, :], pos[:, :], P.bit_length() - 1, None, ALU.logical_shift_right))
            nc.vector.tensor_copy(pos_rowf[:, :], pos_row[:, :])
            link(nc.vector.tensor_tensor(slot_eq[:, :, :], iota_s[:, :].unsqueeze(1).to_broadcast([P, TILES, ST]),
                                         pos_slot[:, :].unsqueeze(2).to_broadcast([P, TILES, ST]), ALU.is_equal))
            nc.vector.tensor_tensor(slot_token[:, :, :], slot_eq[:, :, :],
                                    token1[:, :].unsqueeze(2).to_broadcast([P, TILES, ST]), ALU.mult
                                    ).then_inc(slot_ready, 1)
            for t in range(TILES):
                nc.vector.tensor_scalar(row_onehot[:, t, :], iota_r[:, :], pos_rowf[:, t:t + 1], None, ALU.is_equal
                                        ).then_inc(onehot_ready, 1)
            link(nc.vector.tensor_tensor(done_e[:, :, :], last[0:1, :].unsqueeze(1).to_broadcast([1, ST, E]),
                                         iota_s[0:1, :].unsqueeze(2).to_broadcast([1, ST, E]), ALU.is_le))
            link(nc.vector.reduce_sum(slot_ef[:, :], done_e[:, :, :], AXX))
            for table, width in ((slot_w, WE), (slot_b1, FC), (slot_b2, D)):
                ins = nc.vector.tensor_scalar(table[:, :], slot_ef[:, :], float(E - 1), float(width), ALU.min, ALU.mult)
            ins.then_inc(table_ready, 1)
            dve.wait_ge(inv_ready, 1)
            nc.vector.tensor_copy(from_row[:, :], ps_inv).then_inc(index_ready, 1)
            link(nc.vector.tensor_scalar(empty[:, :], ps_inv, 0.0, FAR, ALU.is_equal, ALU.mult))
            nc.vector.scalar_tensor_tensor(to_row[:, :], ps_inv, -1.0, empty[:, :], ALU.add, ALU.add
                                           ).then_inc(index_ready, 1)

            def col(s, c, n=1):
                return gathered[:, s * ROW + c:s * ROW + c + n]

            def slot_norm(s):
                dve.wait_ge(landed, s + 1)
                if s >= 2:
                    dve.wait_ge(fT_ready, s - 1)
                nc.vector.tensor_scalar(xs[s % 2], col(s, 0, D), col(s, MEAN), col(s, RSTD),
                                        ALU.subtract, ALU.mult).then_inc(xs_ready, 1)

            def x_low(s):
                dve.wait_ge(xhi_ready, s + 1)
                nc.vector.scalar_tensor_tensor(x_lo[s % 2], ps_x[s % 2], XS, x_hi[s % 2], ALU.mult, ALU.subtract
                                               ).then_inc(xlo_ready, 1)

            def h_split(s, half):
                q, part = s % 2, slice(half * F // 2, (half + 1) * F // 2)
                dve.wait_ge(gelu_ready, 2 * s + half + 1)
                if s >= 2:
                    dve.wait_ge(mm2_ready, s - 1)
                nc.vector.tensor_scalar(h_hi[q][:, part], h[:, part], HS, None, ALU.mult).then_inc(hhi_ready, 1)
                dve.wait_ge(hhi_ready, 2 * s + half + 1)
                nc.vector.scalar_tensor_tensor(h_lo[q][:, part], h[:, part], HS, h_hi[q][:, part],
                                               ALU.mult, ALU.subtract).then_inc(hlo_ready, 1)

            def finish(s):
                q = s % 2
                if s >= 1:
                    dve.wait_ge(out_ready, s)
                dve.wait_ge(mm2_ready, s + 1)
                nc.vector.scalar_tensor_tensor(y_sb[:, :], ps_y[q][:, 0:D], 1.0 / (HS * WS),
                                               b2_rep[:, bass.ds(b2_at[s], D)], ALU.mult, ALU.add).then_inc(y_half, 1)
                dve.wait_ge(y_half, s + 1)
                nc.vector.scalar_tensor_tensor(y_sb[:, :], ps_y[q][:, D:2 * D], 1.0 / (HS * WS), y_sb[:, :],
                                               ALU.mult, ALU.add).then_inc(y_ready, 1)
                dve.wait_ge(y_ready, s + 1)
                if s >= 2:
                    dve.wait_ge(stored[q], 16 * (s // 2))
                nc.vector.scalar_tensor_tensor(out_sb[q], y_sb[:, :], col(s, PMAX), col(s, 0, D),
                                               ALU.mult, ALU.add).then_inc(out_ready, 1)

            dve.wait_ge(b2_in, 16)
            dve.wait_ge(table_ready, 1)
            b2_at = slot_offsets(slot_b2, mybir.EngineType.DVE, D)
            slot_norm(0)
            slot_norm(1)
            x_low(0)
            x_low(1)
            slot_norm(2)
            h_split(0, 0)
            for s in range(SLOTS):
                h_split(s, 1)
                if s + 2 < SLOTS:
                    x_low(s + 2)
                if s >= 1:
                    finish(s - 1)
                if s + 1 < SLOTS:
                    h_split(s + 1, 0)
                if s + 3 < SLOTS:
                    slot_norm(s + 3)
            finish(SLOTS - 1)


SPLIT_ACT = (3, 3, 2)
SPLIT_DVE = (4, 4)
STORE_AT = 20
AHEAD = 4

_INS = ["x", "ctx_1024", "L0_xattn_Wq", "L0_xattn_bq", "L0_xattn_Wk", "L0_xattn_bk", "L0_ffn_Wr", "L0_ffn_W1",
        "L0_ffn_b1", "L0_ffn_W2", "L0_ffn_b2"]


def kernel(**inputs):
    import numpy as _np
    import concourse.bacc as _bacc
    from concourse import mybir as _mybir
    from concourse.bass_utils import run_bass_kernel_spmd as _run

    nc = _bacc.Bacc("TRN2", target_bir_lowering=False, num_devices=1)
    arrays, args = {}, []
    for name in _INS:
        a = _np.ascontiguousarray(inputs[name])
        arrays[f"in_{name}_dram"] = a
        args.append(nc.dram_tensor(f"in_{name}_dram", a.shape, _mybir.dt.from_np(a.dtype), kind="ExternalInput").ap())
    args.append(nc.dram_tensor("out_0_dram", (B, S, D), F32, kind="ExternalOutput").ap())
    build(nc, *args)
    r = _run(nc, [arrays], core_ids=[0])
    return r.results[0]["out_0_dram"]
```

```python
from contextlib import ExitStack

import concourse.bass as bass
from concourse import mybir

ALU = mybir.AluOpType
ACT = mybir.ActivationFunctionType
AXX = mybir.AxisListType.X
F32 = mybir.dt.float32
F16 = mybir.dt.float16
I32 = mybir.dt.int32

P = 128
D = 256
KD = D // P
B, S = 2, 1024
CTX = 77
E, F = 8, 1024
FC = F // P
TOKENS = B * S
TILES = TOKENS // P
TPB = S // P
GT = 4
GROUPS = TILES // GT
SLOTS = (TOKENS + E * (P - 1)) // P
MIN_SLOTS = TOKENS // P
IN_USE, IN_TIME = SLOTS, SLOTS + 1
ST = SLOTS + 2
ROW = D + 4
MEAN, RSTD, PMAX = D, D + 1, D + 2
EPS = 1e-5
ATT_SCALE = 1.0 / 32.0
XS = 64.0
WS = 64.0
HS = 16.0
WE = 2 * KD * F
PIECE = 1024
PIECES = E * 4
RING = 6
LATE_RING = 4
FAR = 8192.0


def build(nc, x, ctx, wq, bq, wk, bk, wr, w1, b1, w2, b2, out):
    assert SLOTS >= E and (TOKENS + 1) < FAR
    with ExitStack() as stack:
        def sb(name, shape, dt=F32):
            return stack.enter_context(nc.sbuf_tensor(name, shape, dt))

        def sem(name):
            return stack.enter_context(nc.semaphore(name))

        scratch = nc.dram_tensor("token_rows", [TOKENS + 1, ROW], F32, kind="Internal").ap()

        w1_pair = sb("w1_pair", [P, E * WE], F16)
        w2_pair = sb("w2_pair", [P, E * WE], F16)
        stage = sb("stage", [P, LATE_RING, PIECE])
        b2_rep = sb("b2_rep", [P, E * D])
        b1_T = sb("b1_T", [P, E * FC])
        gathered = sb("gathered", [P, SLOTS * ROW])
        xT = [gathered[:, g * 1024:(g + 1) * 1024].rearrange("p (k n) -> p k n", k=KD) for g in range(GROUPS)]
        probs = gathered[:, 4096:4096 + GT * 80].rearrange("p (j c) -> p j c", j=GT)
        wq_sb = gathered[:, 4416:4928].rearrange("p (k d) -> p k d", k=KD)
        wk_sb = gathered[:, 4928:5440].rearrange("p (k d) -> p k d", k=KD)
        row_onehot = gathered[:, 4416:5440].bitcast(F16).rearrange("p (t r) -> p t r", t=TILES)
        wkT = gathered[:, 5440:5952].rearrange("p (k d) -> p k d", k=KD)
        scaled = gathered[:, 5440:5440 + GT * CTX].rearrange("p (j c) -> p j c", j=GT)
        rows = sb("rows", [P, TILES, ROW])
        rows_flat = rows[:, :, :].rearrange("p t r -> p (t r)")
        h = rows_flat[:, 0:F]
        xs = rows_flat[:, F:F + D]
        x_pair = [rows_flat[:, F + (2 + i) * D:F + (3 + i) * D].bitcast(F16) for i in range(2)]
        x_hi = [pair[:, 0:D] for pair in x_pair]
        x_lo = [pair[:, D:2 * D] for pair in x_pair]
        h_hi = [rows_flat[:, 2048 + i * 512:2560 + i * 512].bitcast(F16) for i in range(2)]
        h_lo = [rows_flat[:, 3072 + i * 512:3584 + i * 512].bitcast(F16) for i in range(2)]

        ident = sb("ident", [P, P])
        ident16 = sb("ident16", [P, P], F16)
        before = sb("before", [P, P], F16)
        ones16 = sb("ones16", [P, P], F16)
        ones8 = sb("ones8", [P, E])
        iota_r = sb("iota_r", [P, P], F16)
        iota_s = sb("iota_s", [P, ST], I32)
        token1 = sb("token1", [P, TILES])
        rev = sb("rev", [P, E])
        steps128 = sb("steps128", [P, TILES - 1])
        not_first = sb("not_first", [P, E * TILES])
        neg_half = sb("neg_half", [P, GT])
        neg_mean = gathered[:, 3816:3944]
        zero_row = sb("zero_row", [1, ROW])

        ctx_sb = sb("ctx_sb", [CTX, B, D + E])
        ctxT = gathered[:, 3072:3380].rearrange("p (k c) -> p k c", k=KD)
        kT = gathered[:, 3380:3688].rearrange("p (k c) -> p k c", k=KD)
        qkT = sb("qkT", [P, KD, B, CTX + E])
        x_rows = [rows_flat[:, F + D:F + 2 * D].bitcast(F16),
                  qkT[:, :, :, :].rearrange("p k b c -> p (k b c)")[:, 0:D].bitcast(F16)]
        qbias = sb("qbias", [P, B * CTX])
        wq_stats = sb("wq_stats", [P, KD, 6])
        wq_mean = sb("wq_mean", [P, KD, 2])
        logit_x = sb("logit_x", [P, TILES, E])
        logits = sb("logits", [P, TILES, E])
        bq_sb = sb("bq_sb", [P, KD])
        bk_sb = sb("bk_sb", [P, KD])
        b1_sb = gathered[0:E * FC, 3688:3688 + P]
        wr_sb = sb("wr_sb", [P, KD, E])
        probsT = sb("probsT", [P, GT * P])
        stats = sb("stats", [P, GT, 6])
        smax = sb("smax", [P, GT])
        nbias = sb("nbias", [P, GT])
        ssum = sb("ssum", [P, TILES])
        rsum = sb("rsum", [P, GT])

        lmax = sb("lmax", [P, TPB])
        ldiff = sb("ldiff", [P, TPB, E])
        lscaled = sb("lscaled", [P, TPB, E])
        lexp = sb("lexp", [P, TPB, E])
        lrev = sb("lrev", [P, TPB, E])
        lrmax = sb("lrmax", [P, TPB])
        lsum = sb("lsum", [P, TPB])
        chosen = sb("chosen", [P, E, TILES], F16)
        upto = gathered[:, 4096:4224]
        place = gathered[:, 4224:4352]
        more = sb("more", [P, E, TILES - 1])
        extra = sb("extra", [P, E])
        last = sb("last", [P, E])
        base = sb("base", [P, E])
        pos = sb("pos", [P, TILES], I32)
        pos_row = sb("pos_row", [P, TILES], I32)
        pos_rowf = sb("pos_rowf", [P, TILES])
        pos_slot = sb("pos_slot", [P, TILES], I32)
        slot_eq = gathered[:, 0:TILES * ST // 2].bitcast(F16).rearrange("p (t s) -> p t s", t=TILES)
        done_e = sb("done_e", [1, ST, E])
        slot_ef = sb("slot_ef", [1, ST])
        late_first = sb("late_first", [1, len(LATE_FIRST)])
        late_ok = sb("late_ok", [1, len(LATE_FIRST)])
        in_time_f = sb("in_time_f", [1, 1])
        slot_w = sb("slot_w", [1, ST], I32)
        slot_b1 = sb("slot_b1", [1, ST], I32)
        slot_b2 = sb("slot_b2", [1, ST], I32)
        empty = sb("empty", [P, ST])
        from_row = sb("from_row", [P, ST], I32)
        to_row = sb("to_row", [P, ST], I32)

        out_sb = [probsT[:, i * D:(i + 1) * D] for i in range(2)]
        y_sb = sb("y_sb", [P, D])

        psum = stack.enter_context(nc.psum_tensor("psum", [P, 8, 512], F32))
        bank = [psum[:, i, :] for i in range(8)]
        ps_xT = [bank[0], bank[1]]
        ps_pT = bank[2]
        ps_sc = bank[3].rearrange("p (j c) -> p j c", j=GT)
        ps_att = psum[:, 4:4 + GT, 0:D + E]
        ps_rank = bank[3][:, 128:256]
        ps_total = bank[3][:, 256:384]
        ps_inv = bank[3][:, 384:384 + ST]
        ps_h = [[bank[0], bank[1]], [bank[2], bank[3]]]
        ps_x = [bank[4].bitcast(F16)[:, 0:2 * D], bank[6].bitcast(F16)[:, 0:2 * D]]
        ps_y = [bank[5], bank[7]]

        ctx_in, wk_in, wq_in, small_in, b1_in, b2_in = (sem(n) for n in (
            "ctx_in", "wk_in", "wq_in", "small_in", "b1_in", "b2_in"))
        x_in = [sem(f"x_in{g}") for g in range(GROUPS)]
        piece_in = [sem(f"piece_in{r}") for r in range(RING)]
        rows_out = [sem(f"rows_out{b}") for b in range(B)]
        zero_out = sem("zero_out")
        filled, consts = sem("filled"), sem("consts")
        setup_T, setup_TC, setup_k, setup_kC, setup_q, setup_qC = (sem(n) for n in (
            "setup_T", "setup_TC", "setup_k", "setup_kC", "setup_q", "setup_qC"))
        wq_centred, wr_mean_ready, wr_centred, ctx_wr_ready, ctx_wr_copied = (sem(n) for n in (
            "wq_centred", "wr_mean_ready", "wr_centred", "ctx_wr_ready", "ctx_wr_copied"))
        b1_T_ready, b1_T_copied = sem("b1_T_ready"), sem("b1_T_copied")
        piece_hi = sem("piece_hi")
        lo_by_dve, lo_by_pool, piece_scaled = sem("lo_by_dve"), sem("lo_by_pool"), sem("piece_scaled")
        var_ready, rstd_ready, xT_ready, xT_copied = (sem(n) for n in (
            "var_ready", "rstd_ready", "xT_ready", "xT_copied"))
        score_ready, nbias_ready, exp_ready, probs_ready, pT_ready, pT_copied, att_ready, x1_ready = (
            sem(n) for n in ("score_ready", "nbias_ready", "exp_ready", "probs_ready", "pT_ready", "pT_copied",
                             "att_ready", "x1_ready"))
        logits_ready = sem("logits_ready")
        ldiff_ready, lexp_ready, rows_ready, chosen_ready, rank_ready = (sem(n) for n in (
            "ldiff_ready", "lexp_ready", "rows_ready", "chosen_ready", "rank_ready"))
        slot_ready, onehot_ready, onehot_by_pool, inv_ready, index_ready, table_ready = (sem(n) for n in (
            "slot_ready", "onehot_ready", "onehot_by_pool", "inv_ready", "index_ready", "table_ready"))
        dve_step = sem("dve_step")
        got = [sem(f"got{i}") for i in range(AHEAD)]
        landed = sem("landed")
        stored = [sem(f"stored{i}") for i in range(2)]
        xs_ready, fT_ready, xhi_ready, xlo_ready, mm1_ready, gelu_ready = (sem(n) for n in (
            "xs_ready", "fT_ready", "xhi_ready", "xlo_ready", "mm1_ready", "gelu_ready"))
        hhi_ready, hlo_ready, mm2_ready, y_ready, out_ready = (sem(n) for n in (
            "hhi_ready", "hlo_ready", "mm2_ready", "y_ready", "out_ready"))
        y_half = sem("y_half")
        xT_pair_copied = sem("xT_pair_copied")

        x_v = x.rearrange("b (p i j) d -> b i p j d", p=P, j=GT)
        rows_v = scratch[1:TOKENS + 1, :].rearrange("(b p j) r -> b p j r", b=B, p=P)
        out_rows = out.rearrange("b s d -> (b s) d")

        def place_of(i):
            if i >= EARLY_PIECES:
                return (i - EARLY_PIECES) % LATE_RING
            if i in POOL_PIECES:
                return LATE_RING + POOL_PIECES.index(i) % (RING - LATE_RING)
            return sum(n not in POOL_PIECES for n in range(i)) % LATE_RING

        def before_in_place(i):
            return max((n for n in range(i) if place_of(n) == place_of(i)), default=None)

        def piece_views(i):
            at = place_of(i)
            place = (stage[:, at, :] if at < LATE_RING
                     else b2_rep[:, (at - LATE_RING) * PIECE:(at - LATE_RING + 1) * PIECE])
            e, kind = divmod(i, 4)
            if kind < 2:
                src = w1[e, kind * P:(kind + 1) * P, :]
                at = e * WE + kind * F
                return src, place, w1_pair[:, at:at + F], w1_pair[:, at + KD * F:at + (KD + 1) * F]
            half = (kind - 2) * (F // 2)
            src = w2[e, half:half + F // 2, :].rearrange("(c p) d -> p c d", p=P)
            at = e * WE + (kind - 2) * 2 * PIECE
            pair = w2_pair[:, at:at + 2 * PIECE].rearrange("p (c t d) -> p c t d", t=2, d=D)
            return src, place.rearrange("p (c d) -> p c d", d=D), pair[:, :, 0, :], pair[:, :, 1, :]

        def wait_split(engine, i):
            if i in POOL_PIECES:
                engine.wait_ge(lo_by_pool, POOL_PIECES.index(i) + 1)
            else:
                engine.wait_ge(lo_by_dve, sum(n not in POOL_PIECES for n in range(i + 1)))

        def wait_lo(engine, i):
            by_pool = sum(1 for n in range(i + 1) if n in POOL_PIECES)
            if by_pool:
                engine.wait_ge(lo_by_pool, by_pool)
            if i + 1 - by_pool:
                engine.wait_ge(lo_by_dve, i + 1 - by_pool)

        STATS = [("x", g) for g in range(GROUPS)] + [("x1", g) for g in range(GROUPS)]
        seq_of = {key: n for n, key in enumerate(STATS)}

        block = stack.enter_context(nc.Block())

        def slot_offsets(table, engine, width):
            _, values = nc.values_load_multi_w_load_instructions(
                table[0:1, 0:ST], engines=[engine], min_val=0, max_val=(E - 1) * width,
                skip_runtime_bounds_check_because="the table is clamped to the last expert where it is written")
            return values[:SLOTS], values[IN_USE], values[IN_TIME]

        def steps_in_use(engine, in_use, step, last_step):
            def from_step(s):
                if s + 1 == SLOTS:
                    last_step(s)
                    return
                with engine.If(in_use > s + 1):
                    step(s)
                    from_step(s + 1)
                with engine.Else():
                    last_step(s)

            for s in range(MIN_SLOTS - 1):
                step(s)
            from_step(MIN_SLOTS - 1)

        @block.sync
        def _(sp):
            def load_x(g):
                b, i = divmod(g, TPB // GT)
                sp.dma_start(rows[:, g * GT:(g + 1) * GT, 0:D], x_v[b, i]).then_inc(x_in[g], 16)

            sp.dma_start(wk_sb, wk.rearrange("(k p) d -> p k d", p=P)).then_inc(wk_in, 16)
            sp.dma_start(ctx_sb[:, :, 0:D], ctx.rearrange("b c d -> c b d")).then_inc(ctx_in, 16)
            sp.dma_start(wq_sb, wq.rearrange("(k p) d -> p k d", p=P)).then_inc(wq_in, 16)
            load_x(0)
            sp.dma_start(wr_sb[:, :, :], wr.rearrange("(k p) e -> p k e", p=P)).then_inc(small_in, 16)
            with nc.allow_non_contiguous_dma(reason="two bias vectors of 256 elements"):
                sp.dma_start(bk_sb[:, :], bk.rearrange("(k p) -> p k", p=P)).then_inc(small_in, 16)
                sp.dma_start(bq_sb[:, :], bq.rearrange("(k p) -> p k", p=P)).then_inc(small_in, 16)
            sp.dma_start(b1_sb, b1.rearrange("e (c p) -> (e c) p", p=P)).then_inc(b1_in, 16)

            def load_piece(i):
                if before_in_place(i) is not None:
                    wait_split(sp, before_in_place(i))
                src, dst, _, _ = piece_views(i)
                sp.dma_start(dst, src).then_inc(piece_in[place_of(i)], 16)

            def store_tiles(first, last, cols):
                b = first // TPB
                sp.dma_start(rows_v[b][:, first - b * TPB:last - b * TPB, cols], rows[:, first:last, cols]
                             ).then_inc(rows_out[b], 16)

            def relay(s):
                sp.wait_ge(got[s % AHEAD], 16 * (s // AHEAD + 1))
                sp.sem_inc(landed, 1)

            for i in range(EARLY_PIECES + LATE_RING):
                if i == EARLY_PIECES:
                    sp.wait_ge(rows_ready, 1)
                    store_tiles(0, TPB, slice(0, ROW))
                load_piece(i)
                if i in LOAD_X_AFTER:
                    load_x(1 + LOAD_X_AFTER.index(i))
                if i == RING:
                    sp.wait_ge(filled, 1)
                    sp.dma_start(scratch[0:1, :], zero_row[:, :]).then_inc(zero_out, 16)
            sp.wait_ge(rstd_ready, seq_of["x1", GROUPS - 2] + 1)
            store_tiles(TPB, TILES - GT, slice(0, PMAX))
            wait_lo(sp, EARLY_PIECES - 1)
            sp.dma_start(b2_rep[:, :], b2.rearrange("e d -> (e d)").partition_broadcast(P)).then_inc(b2_in, 16)
            sp.wait_ge(rows_ready, 2)
            store_tiles(TILES - GT, TILES, slice(0, ROW))
            store_tiles(TPB, TILES - GT, slice(PMAX, ROW))
            for s in range(AHEAD + 2):
                relay(s)
            more = range(EARLY_PIECES + LATE_RING, PIECES)
            sp.wait_ge(table_ready, 1)
            _, (in_time,) = nc.values_load_multi_w_load_instructions(
                slot_b1[0:1, IN_TIME:ST], engines=[mybir.EngineType.SP], min_val=0, max_val=len(LATE_FIRST),
                skip_runtime_bounds_check_because="it counts the late experts")
            with sp.If(in_time > len(LATE_FIRST) - 1):
                for s in range(AHEAD + 2, SLOTS):
                    if s - AHEAD - 2 < len(more):
                        load_piece(more[s - AHEAD - 2])
                    relay(s)
            with sp.Else():
                for i in more:
                    load_piece(i)
                for s in range(AHEAD + 2, SLOTS):
                    relay(s)

        @block.gpsimd
        def _(pool):
            pool.memset(zero_row[:, :], 0.0)
            pool.memset(ident[:, :], 0.0)
            pool.memset(before[:, :], 1.0)
            pool.memset(ident16[:, :], 0.0)
            pool.memset(not_first[:, :], 1.0)
            pool.memset(ones16[:, :], 1.0)
            pool.memset(neg_mean, -1.0 / D)
            pool.memset(ones8[:, :], 1.0)
            pool.memset(neg_half[:, :], -0.5).then_inc(filled, 1)
            pool.wait_ge(filled, 1)
            pool.affine_select(out=ident[:, :], in_=ident[:, :], pattern=[[-1, P]], compare_op=ALU.not_equal,
                               fill=1.0, base=0, channel_multiplier=1).then_inc(consts, 1)
            pool.affine_select(out=ident16[:, :], in_=ident16[:, :], pattern=[[-1, P]], compare_op=ALU.not_equal,
                               fill=1.0, base=0, channel_multiplier=1)
            pool.affine_select(out=before[:, :], in_=before[:, :], pattern=[[1, P]], compare_op=ALU.is_gt,
                               fill=0.0, base=0, channel_multiplier=-1)
            nf = not_first[:, :].rearrange("p (e t) -> p e t", e=E)
            pool.affine_select(out=nf, in_=nf, pattern=[[0, E], [1, TILES]], compare_op=ALU.is_gt,
                               fill=0.0, base=0, channel_multiplier=0)
            pool.iota(iota_r[:, :], pattern=[[1, P]], base=0, channel_multiplier=0,
                      allow_small_or_imprecise_dtypes=True)
            pool.iota(iota_s[:, :], pattern=[[1, ST]], base=0, channel_multiplier=0)
            pool.iota(token1[:, :].rearrange("p (b j) -> p b j", b=B), pattern=[[S, B], [1, TPB]], base=1,
                      channel_multiplier=TPB, allow_small_or_imprecise_dtypes=True)
            pool.iota(late_first[:, :], pattern=[[4, len(LATE_FIRST)]], base=LATE_FIRST[0], channel_multiplier=0,
                      allow_small_or_imprecise_dtypes=True)
            pool.iota(rev[:, :], pattern=[[-1, E]], base=E, channel_multiplier=0,
                      allow_small_or_imprecise_dtypes=True)
            pool.iota(steps128[:, :], pattern=[[P, TILES - 1]], base=P, channel_multiplier=0,
                      allow_small_or_imprecise_dtypes=True).then_inc(consts, 1)

            pieces = list(POOL_PIECES)

            def split(n):
                for _ in range(min(n, len(pieces))):
                    i = pieces.pop(0)
                    _, st, hi, lo = piece_views(i)
                    pool.wait_ge(piece_hi, i + 1)
                    pool.tensor_tensor(lo, st, hi, ALU.subtract).then_inc(lo_by_pool, 1)

            for n, (_, g) in enumerate(STATS):
                pool.wait_ge(var_ready, n + 1)
                pool.tensor_tensor(rows[:, g * GT:(g + 1) * GT, RSTD], rows[:, g * GT:(g + 1) * GT, RSTD],
                                   neg_half[:, :], ALU.pow).then_inc(rstd_ready, 1)
                split(SPLIT_POOL[n])

            def gather(s):
                pool.indirect_dma_start(
                    out=gathered[:, s * ROW:(s + 1) * ROW], out_offset=None, in_=scratch[:, :],
                    in_offset=bass.IndirectOffsetOnAxis(ap=from_row[:, s:s + 1], axis=0),
                    bounds_check=TOKENS, oob_is_err=False).then_inc(got[s % AHEAD], 16)

            pool.wait_ge(slot_ready, 1)
            for t in range(DVE_ONEHOTS, TILES):
                pool.tensor_scalar(row_onehot[:, t, :], iota_r[:, :], pos_rowf[:, t:t + 1], token1[:, t:t + 1],
                                   ALU.is_equal, ALU.mult).then_inc(onehot_by_pool, 1)

            pool.wait_ge(index_ready, 2)
            pool.wait_ge(zero_out, 16)
            pool.wait_ge(rows_out[0], 16)
            pool.wait_ge(rows_out[1], 3 * 16)
            for s in range(AHEAD):
                gather(s)
            pool.wait_ge(table_ready, 1)
            _, (in_use,) = nc.values_load_multi_w_load_instructions(
                slot_b1[0:1, IN_USE:IN_USE + 1], engines=[mybir.EngineType.Pool], min_val=MIN_SLOTS, max_val=SLOTS,
                skip_runtime_bounds_check_because="the number of slots is bounded by the shapes")

            def scatter(s):
                pool.wait_ge(out_ready, s + 1)
                pool.indirect_dma_start(
                    out=out_rows, out_offset=bass.IndirectOffsetOnAxis(ap=to_row[:, s:s + 1], axis=0),
                    in_=out_sb[s % 2], in_offset=None,
                    bounds_check=TOKENS - 1, oob_is_err=False).then_inc(stored[s % 2], 16)

            def step(s):
                for n in range(AHEAD + 2 * s, AHEAD + 2 * s + 2):
                    if n < SLOTS:
                        pool.wait_ge(got[n % AHEAD], 16 * (n // AHEAD))
                        gather(n)
                scatter(s)

            def last_step(s):
                scatter(s)
                for q in range(2):
                    pool.wait_ge(stored[q], 16 * ((s + 2 - q) // 2))

            steps_in_use(pool, in_use, step, last_step)

        @block.scalar
        def _(act):
            def copy_xT(g):
                act.wait_ge(xT_ready, g + 1)
                for k in range(KD):
                    ins = nc.scalar.copy(xT[g][:, k, :], ps_xT[k][:, :])
                ins.then_inc(xT_copied, 1)

            def split_hi(i):
                _, st, hi, _ = piece_views(i)
                act.wait_ge(piece_in[place_of(i)], 16 * sum(place_of(n) == place_of(i) for n in range(i + 1)))
                if i in POOL_PIECES:
                    nc.scalar.activation(st, st, ACT.Copy, scale=WS).then_inc(piece_scaled, 1)
                    act.wait_ge(piece_scaled, POOL_PIECES.index(i) + 1)
                    nc.scalar.activation(hi, st, ACT.Copy).then_inc(piece_hi, 1)
                else:
                    nc.scalar.activation(hi, st, ACT.Copy, scale=WS).then_inc(piece_hi, 1)

            todo = list(range(EARLY_PIECES))

            def split(n):
                for _ in range(min(n, len(todo))):
                    split_hi(todo.pop(0))

            act.wait_ge(setup_T, 1)
            nc.scalar.copy(wkT[:, 0, :], bank[0][:, 0:D])
            nc.scalar.copy(wkT[:, 1, :], bank[1][:, 0:D])
            for b in range(B):
                nc.scalar.copy(ctxT[:, :, b * CTX:(b + 1) * CTX],
                               bank[2][:, b * 2 * CTX:(b + 1) * 2 * CTX].rearrange("p (k c) -> p k c", k=KD)
                               ).then_inc(setup_TC, 1)
            act.wait_ge(setup_k, 1)
            act.wait_ge(small_in, 48)
            for k in range(KD):
                ins = nc.scalar.activation(kT[:, k, :], bank[5][:, k * B * CTX:(k + 1) * B * CTX], ACT.Identity,
                                           bias=bk_sb[:, k:k + 1])
            ins.then_inc(setup_kC, 1)
            copy_xT(0)
            split(FIRST_ACT[0])
            act.wait_ge(setup_q, 1)
            for k in range(KD):
                nc.scalar.copy(qkT[:, k, :, 0:CTX], bank[7][:, k * B * CTX:(k + 1) * B * CTX]
                               .rearrange("p (b c) -> p b c", b=B))
            nc.scalar.copy(qbias[:, :], bank[6][:, 0:B * CTX]).then_inc(setup_qC, 1)
            act.wait_ge(ctx_wr_ready, 1)
            nc.scalar.copy(ctx_sb[:, :, D:D + E], bank[5][0:CTX, 0:B * E].rearrange("c (b e) -> c b e", e=E)
                           ).then_inc(ctx_wr_copied, 1)

            def exps(g):
                act.wait_ge(nbias_ready, g + 1)
                if g:
                    act.wait_ge(pT_ready, g)
                for j in range(GT):
                    ins = nc.scalar.activation(probs[:, j, 0:CTX], scaled[:, j, :], ACT.Exp,
                                               bias=nbias[:, j:j + 1], scale=ATT_SCALE,
                                               accum_out=ssum[:, g * GT + j:g * GT + j + 1])
                ins.then_inc(exp_ready, 1)

            def copy_pT(g):
                act.wait_ge(pT_ready, g + 1)
                if g:
                    act.wait_ge(att_ready, g)
                nc.scalar.copy(probsT[0:CTX, :], ps_pT[0:CTX, :]).then_inc(pT_copied, 1)

            def logit_exp(b):
                act.wait_ge(ldiff_ready, b + 1)
                nc.scalar.activation(lexp[:, :, :], lscaled[:, :, :], ACT.Exp).then_inc(lexp_ready, 1)

            split(FIRST_ACT[1])
            copy_xT(1)
            act.wait_ge(b1_T_ready, 1)
            nc.scalar.copy(b1_T[:, :], bank[7][:, 0:E * FC]).then_inc(b1_T_copied, 1)
            split(FIRST_ACT[2])
            for g in range(GROUPS):
                if g == GROUPS - 1:
                    logit_exp(0)
                exps(g)
                if g + 2 < GROUPS:
                    copy_xT(g + 2)
                split(SPLIT_ACT[g][0])
                copy_pT(g)
                split(SPLIT_ACT[g][1])
            split(len(todo))
            logit_exp(1)

            def x_high(s):
                act.wait_ge(xs_ready, s + 1)
                if s >= 2:
                    act.wait_ge(fT_ready, s - 1)
                nc.scalar.activation(x_rows[s % 2][:, 0:D], xs, ACT.Copy, scale=XS).then_inc(xhi_ready, 1)

            def copy_pair(s):
                act.wait_ge(fT_ready, s + 1)
                if s >= 2:
                    act.wait_ge(mm1_ready, 2 * s - 2)
                nc.scalar.copy(x_pair[s % 2], ps_x[s % 2]).then_inc(xT_pair_copied, 1)

            def gelus(s, half):
                q = s % 2
                act.wait_ge(mm1_ready, 2 * s + half + 1)
                if s >= 1:
                    act.wait_ge(hlo_ready, 2 * s - 1 + half)
                for c in range(half * 4, half * 4 + 4):
                    ins = nc.scalar.activation(h[:, c * P:(c + 1) * P], ps_h[q][half][:, (c % 4) * P:(c % 4 + 1) * P],
                                               ACT.Gelu, bias=b1_T[:, bass.ds(b1_at[s] + c, 1)],
                                               scale=1.0 / (XS * WS))
                ins.then_inc(gelu_ready, 1)

            act.wait_ge(chosen_ready, 2)
            nc.scalar.activation(nbias[:, 0:1], nbias[:, 1:2], ACT.Gelu)
            act.wait_ge(table_ready, 1)
            b1_at, in_use, in_time = slot_offsets(slot_b1, mybir.EngineType.Activation, FC)
            x_high(0)
            copy_pair(0)
            x_high(1)
            copy_pair(1)
            x_high(2)
            gelus(0, 0)
            def step(s):
                gelus(s, 1)
                if s + 2 < SLOTS:
                    copy_pair(s + 2)
                if s + 3 < SLOTS:
                    x_high(s + 3)
                gelus(s + 1, 0)

            def step_and_split(s):
                step(s)
                if EARLY_PIECES + s < PIECES:
                    split_hi(EARLY_PIECES + s)

            with act.If(in_time > len(LATE_FIRST) - 1):
                steps_in_use(act, in_use, step_and_split, lambda s: gelus(s, 1))
            with act.Else():
                for i in range(EARLY_PIECES, PIECES):
                    split_hi(i)
                steps_in_use(act, in_use, step, lambda s: gelus(s, 1))

        @block.tensor
        def _(pe):
            def mm(o, lhsT, rhs, start, stop):
                return nc.tensor.matmul(o, lhsT, rhs, start=start, stop=stop)

            def transposes(g):
                pe.wait_ge(x_in[g], 16)
                if g:
                    pe.wait_ge(xT_copied, g)
                else:
                    pe.wait_ge(setup_TC, B)
                for k in range(KD):
                    for j in range(GT):
                        ins = nc.tensor.transpose(ps_xT[k][:, j * P:(j + 1) * P],
                                                  rows[:, g * GT + j, k * P:(k + 1) * P], ident[:, :])
                ins.then_inc(xT_ready, 1)

            pe.wait_ge(consts, 1)
            pe.wait_ge(wk_in, 16)
            for k in range(KD):
                for m in range(KD):
                    nc.tensor.transpose(bank[k][:, m * P:(m + 1) * P], wk_sb[:, m, k * P:(k + 1) * P], ident[:, :])
            pe.wait_ge(ctx_in, 16)
            for b in range(B):
                for k in range(KD):
                    at = (b * KD + k) * CTX
                    ins = nc.tensor.transpose(bank[2][:, at:at + CTX], ctx_sb[:, b, k * P:(k + 1) * P],
                                              ident[0:CTX, 0:CTX])
            ins.then_inc(setup_T, 1)
            pe.wait_ge(setup_TC, B)
            for m in range(KD):
                for k in range(KD):
                    ins = mm(bank[5][:, m * B * CTX:(m + 1) * B * CTX], wkT[:, k, m * P:(m + 1) * P], ctxT[:, k, :],
                             k == 0, k == KD - 1)
            ins.then_inc(setup_k, 1)

            pe.wait_ge(small_in, 48)
            for k in range(KD):
                ins = mm(bank[4][:, 0:E], neg_mean, wr_sb[:, k, :], k == 0, k == KD - 1)
            ins.then_inc(wr_mean_ready, 1)
            transposes(0)
            pe.wait_ge(setup_kC, 1)
            pe.wait_ge(wq_centred, 1)
            for m in range(KD):
                for k in range(KD):
                    mm(bank[7][:, m * B * CTX:(m + 1) * B * CTX], wq_sb[:, k, m * P:(m + 1) * P], kT[:, k, :],
                       k == 0, k == KD - 1)
            for k in range(KD):
                ins = mm(bank[6][:, 0:B * CTX], bq_sb[:, k:k + 1].to_broadcast([P, P]), kT[:, k, :],
                         k == 0, k == KD - 1)
            ins.then_inc(setup_q, 1)
            pe.wait_ge(wr_centred, 1)
            for b in range(B):
                for k in range(KD):
                    ins = mm(bank[5][0:CTX, b * E:(b + 1) * E], ctxT[:, k, b * CTX:(b + 1) * CTX],
                             wr_sb[:, k, :], k == 0, k == KD - 1)
            ins.then_inc(ctx_wr_ready, 1)

            def scores(g):
                b = g * GT // TPB
                pe.wait_ge(xT_copied, g + 1)
                if g:
                    pe.wait_ge(nbias_ready, g)
                for j in range(GT):
                    for k in range(KD):
                        ins = mm(ps_sc[:, j, 0:CTX + E], xT[g][:, k, j * P:(j + 1) * P], qkT[:, k, b, :],
                                 k == 0, k == KD - 1)
                ins.then_inc(score_ready, 1)

            def probs_T(g):
                pe.wait_ge(probs_ready, g + 1)
                if g:
                    pe.wait_ge(pT_copied, g)
                for j in range(GT):
                    ins = nc.tensor.transpose(ps_pT[0:CTX, j * P:(j + 1) * P], probs[:, j, 0:CTX], ident[:, :])
                ins.then_inc(pT_ready, 1)

            def attend(g):
                b = g * GT // TPB
                pe.wait_ge(pT_copied, g + 1)
                if g:
                    pe.wait_ge(x1_ready, g)
                else:
                    pe.wait_ge(b1_T_copied, 1)
                for j in range(GT):
                    ins = mm(ps_att[:, j, :], probsT[0:CTX, j * P:(j + 1) * P], ctx_sb[:, b, :], True, True)
                ins.then_inc(att_ready, 1)

            pe.wait_ge(setup_qC, 1)
            pe.wait_ge(ctx_wr_copied, 1)
            scores(0)
            transposes(1)
            pe.wait_ge(b1_in, 16)
            nc.tensor.transpose(bank[7][:, 0:E * FC], b1_sb, ident[0:E * FC, 0:E * FC]).then_inc(b1_T_ready, 1)
            transposes(2)
            for g in range(GROUPS):
                if g + 1 < GROUPS:
                    scores(g + 1)
                probs_T(g)
                if g + 3 < GROUPS:
                    transposes(g + 3)
                attend(g)

            pe.wait_ge(chosen_ready, 2)
            pe.wait_ge(consts, 2)
            chosen_all = chosen[:, :, :].rearrange("p e t -> p (e t)")
            mm(ps_rank, before[:, :], chosen_all, True, True)
            mm(ps_total, ones16[:, :], chosen_all, True, True).then_inc(rank_ready, 1)
            pe.wait_ge(slot_ready, 2)
            for t in range(TILES):
                if t < DVE_ONEHOTS:
                    pe.wait_ge(onehot_ready, t + 1)
                else:
                    pe.wait_ge(onehot_by_pool, t + 1 - DVE_ONEHOTS)
                ins = mm(ps_inv, row_onehot[:, t, :], slot_eq[:, t, :], t == 0, t == TILES - 1)
            ins.then_inc(inv_ready, 1)

            def slot_T(s):
                pe.wait_ge(xlo_ready, s + 1)
                if s >= 2:
                    pe.wait_ge(xT_pair_copied, s - 1)
                for n in range(2 * KD):
                    ins = nc.tensor.transpose(ps_x[s % 2][:, n * P:(n + 1) * P],
                                              x_rows[s % 2][:, n * P:(n + 1) * P], ident16[:, :])
                ins.then_inc(fT_ready, 1)

            def w1_at(at, lo, k, c):
                return w1_pair[:, bass.ds(at + (lo * KD * F + k * F + c * P), P)]

            def w2_at(at, c, n):
                return w2_pair[:, bass.ds(at + c * 2 * D, n * D)]

            def addresses(after, this, c):
                if after is not None:
                    for k in range(KD):
                        for lo in range(2):
                            pe.lower_ap(w1_at(after, lo, k, c), for_matmul_weights=True)
                if this is not None:
                    pe.lower_ap(w2_at(this, c - 1, 2))

            def layer1(s, c):
                q = s % 2
                if c == 0:
                    pe.wait_ge(xT_pair_copied, s + 1)
                    if s == 0:
                        wait_lo(pe, EARLY_PIECES - 1)
                    if s in LATE_FIRST:
                        wait_split(pe, EARLY_PIECES + 4 * LATE_FIRST.index(s) + 3)
                if c % 4 == 0 and s >= 2:
                    pe.wait_ge(gelu_ready, 2 * s - 3 + c // 4)
                o = ps_h[q][c // 4][:, (c % 4) * P:(c % 4 + 1) * P]
                terms = [(lo, v, k) for k in range(KD) for lo, v in ((1, x_hi[q]), (0, x_lo[q]), (0, x_hi[q]))]
                for n, (lo, v, k) in enumerate(terms):
                    ins = mm(o, w1_at(w_at[s], lo, k, c), v[:, k * P:(k + 1) * P], n == 0, n == len(terms) - 1)
                if c % 4 == 3:
                    ins.then_inc(mm1_ready, 1)

            def layer2(s, c):
                q, hc = s % 2, slice(c * P, (c + 1) * P)
                if c == 0 and s >= 2:
                    pe.wait_ge(y_ready, s - 1)
                if c % 4 == 0:
                    pe.wait_ge(hlo_ready, 2 * s + c // 4 + 1)
                if c:
                    mm(ps_y[q][:, 0:D], h_lo[q][:, hc], w2_at(w_at[s], c, 1), False, False)
                ins = mm(ps_y[q][:, :], h_hi[q][:, hc], w2_at(w_at[s], c, 2), c == 0, c == FC - 1)
                if c == 0:
                    mm(ps_y[q][:, 0:D], h_lo[q][:, hc], w2_at(w_at[s], c, 1), False, False)
                if c == FC - 1:
                    ins.then_inc(mm2_ready, 1)

            pe.wait_ge(table_ready, 1)
            w_at, in_use, _ = slot_offsets(slot_w, mybir.EngineType.PE, WE)
            slot_T(0)
            for c in range(FC):
                addresses(w_at[0], None, c)
                layer1(0, c)
                if c == 1:
                    slot_T(1)
            def step(s):
                for c in range(FC + 1):
                    addresses(w_at[s + 1] if c < FC else None, w_at[s] if c else None, c)
                    if c < FC:
                        layer1(s + 1, c)
                    if c == 1 and s + 2 < SLOTS:
                        slot_T(s + 2)
                    if c:
                        layer2(s, c - 1)

            def last_step(s):
                for c in range(FC):
                    addresses(None, w_at[s], c + 1)
                    layer2(s, c)

            steps_in_use(pe, in_use, step, last_step)

        @block.vector
        def _(dve):
            steps = [0]

            def link(ins):
                mark(ins)
                until_marked()

            def mark(ins):
                steps[0] += 1
                ins.then_inc(dve_step, 1)

            def until_marked():
                dve.wait_ge(dve_step, steps[0])

            def split_lo(i):
                _, st, hi, lo = piece_views(i)
                dve.wait_ge(piece_hi, i + 1)
                nc.vector.scalar_tensor_tensor(lo, st, WS, hi, ALU.mult, ALU.subtract
                                               ).then_inc(lo_by_dve, 1)

            todo = [i for i in range(EARLY_PIECES) if i not in POOL_PIECES]

            def split(n):
                for _ in range(min(n, len(todo))):
                    split_lo(todo.pop(0))

            def tile_stats(g, j):
                return nc.vector.bn_stats(stats[:, j, :], rows[:, g * GT + j, 0:D])

            def tile_mean(g, j):
                return nc.vector.bn_aggr(rows[:, g * GT + j, MEAN:MEAN + 2], stats[:, j, :])

            def add_eps(g):
                nc.vector.tensor_scalar(rows[:, g * GT:(g + 1) * GT, RSTD], rows[:, g * GT:(g + 1) * GT, RSTD],
                                        EPS, None, ALU.add).then_inc(var_ready, 1)

            def stats_of(g, pieces=0):
                for j in range(GT):
                    ins = tile_stats(g, j)
                mark(ins)
                split(pieces - pieces // 2)
                until_marked()
                for j in range(GT):
                    ins = tile_mean(g, j)
                mark(ins)
                split(pieces // 2)
                until_marked()
                add_eps(g)

            def scale_scores(g):
                cols = slice((g * GT // TPB) * CTX, (g * GT // TPB + 1) * CTX)
                dve.wait_ge(score_ready, g + 1)
                dve.wait_ge(rstd_ready, seq_of["x", g] + 1)
                if g:
                    dve.wait_ge(exp_ready, g)
                for j in range(GT):
                    t = g * GT + j
                    ins = nc.vector.scalar_tensor_tensor(scaled[:, j, :], ps_sc[:, j, 0:CTX],
                                                         rows[:, t, RSTD:RSTD + 1], qbias[:, cols],
                                                         ALU.mult, ALU.add)
                nc.vector.tensor_copy(logit_x[:, g * GT:(g + 1) * GT, :], ps_sc[:, :, CTX:CTX + E])
                link(ins)
                link(nc.vector.reduce_max(smax[:, :], scaled, AXX))
                nc.vector.tensor_scalar(nbias[:, :], smax[:, :], -ATT_SCALE, None, ALU.mult).then_inc(nbias_ready, 1)

            def normalise(g):
                dve.wait_ge(exp_ready, g + 1)
                link(nc.vector.reciprocal(rsum[:, :], ssum[:, g * GT:(g + 1) * GT]))
                nc.vector.tensor_tensor(probs[:, :, 0:CTX], probs[:, :, 0:CTX],
                                        rsum[:, :].unsqueeze(2).to_broadcast([P, GT, CTX]), ALU.mult
                                        ).then_inc(probs_ready, 1)

            def add_logits(g):
                dve.wait_ge(att_ready, g + 1)
                tiles = slice(g * GT, (g + 1) * GT)
                nc.vector.tensor_tensor(logits[:, tiles, :], ps_att[:, :, D:D + E], logit_x[:, tiles, :], ALU.add
                                        ).then_inc(logits_ready, 1)

            def add_attention(g):
                dve.wait_ge(xT_ready, g + 1)
                tiles = slice(g * GT, (g + 1) * GT)
                nc.vector.tensor_tensor(rows[:, tiles, 0:D], ps_att[:, :, 0:D], rows[:, tiles, 0:D], ALU.add
                                        ).then_inc(x1_ready, 1)
                dve.wait_ge(x1_ready, g + 1)

            def route(b):
                tiles = slice(b * TPB, (b + 1) * TPB)
                dve.wait_ge(logits_ready, (b + 1) * TPB // GT)
                link(nc.vector.reduce_max(lmax[:, :], logits[:, tiles, :], AXX))
                link(nc.vector.tensor_tensor(ldiff[:, :, :], logits[:, tiles, :],
                                             lmax[:, :].unsqueeze(2).to_broadcast([P, TPB, E]), ALU.subtract))
                link(nc.vector.scalar_tensor_tensor(lrev[:, :, :], ldiff[:, :, :], 0.0,
                                                    rev[:, :].unsqueeze(1).to_broadcast([P, TPB, E]),
                                                    ALU.is_equal, ALU.mult))
                link(nc.vector.reduce_max(lrmax[:, :], lrev[:, :, :], AXX))
                nc.vector.tensor_tensor(chosen[:, :, tiles].rearrange("p e t -> p t e"), lrev[:, :, :],
                                        lrmax[:, :].unsqueeze(2).to_broadcast([P, TPB, E]),
                                        ALU.is_equal).then_inc(chosen_ready, 1)

            def scale_logits(b):
                tiles = slice(b * TPB, (b + 1) * TPB)
                dve.wait_ge(rstd_ready, seq_of["x1", (b + 1) * TPB // GT - 1] + 1)
                if b:
                    dve.wait_ge(lexp_ready, b)
                nc.vector.tensor_tensor(lscaled[:, :, :], ldiff[:, :, :],
                                        rows[:, tiles, RSTD:RSTD + 1].to_broadcast([P, TPB, E]),
                                        ALU.mult).then_inc(ldiff_ready, 1)

            def largest_prob(b):
                tiles = slice(b * TPB, (b + 1) * TPB)
                dve.wait_ge(lexp_ready, b + 1)
                link(nc.vector.reduce_sum(lsum[:, :], lexp[:, :, :], AXX))
                nc.vector.reciprocal(rows[:, tiles, PMAX], lsum[:, :]).then_inc(rows_ready, 1)

            nc.vector.memset(rows[:, :, PMAX:ROW], 0.0)
            dve.wait_ge(consts, 2)
            dve.wait_ge(wq_in, 16)
            for k in range(KD):
                ins = nc.vector.bn_stats(wq_stats[:, k, :], wq_sb[:, k, :])
            link(ins)
            for k in range(KD):
                ins = nc.vector.bn_aggr(wq_mean[:, k, :], wq_stats[:, k, :])
            link(ins)
            for k in range(KD):
                ins = nc.vector.tensor_scalar(wq_sb[:, k, :], wq_sb[:, k, :], wq_mean[:, k, 0:1], None, ALU.subtract)
            ins.then_inc(wq_centred, 1)
            dve.wait_ge(x_in[0], 16)
            stats_of(0)
            split(FIRST_DVE[0])
            dve.wait_ge(wr_mean_ready, 1)
            link(nc.vector.tensor_tensor(wr_sb[:, :, :], wr_sb[:, :, :],
                                         bank[4][:, 0:E].unsqueeze(1).to_broadcast([P, KD, E]), ALU.add))
            nc.vector.tensor_copy(qkT[:, :, :, CTX:CTX + E], wr_sb[:, :, :].unsqueeze(2).to_broadcast([P, KD, B, E])
                                  ).then_inc(wr_centred, 1)
            for g in range(1, STATS_AHEAD):
                dve.wait_ge(x_in[g], 16)
                stats_of(g, FIRST_DVE[g])
            for g in range(GROUPS):
                if g == 0:
                    dve.wait_ge(setup_qC, 1)
                scale_scores(g)
                if g + STATS_AHEAD < GROUPS:
                    dve.wait_ge(x_in[g + STATS_AHEAD], 16)
                    stats_of(g + STATS_AHEAD)
                if g == GROUPS - 1:
                    largest_prob(0)
                split(SPLIT_DVE[g][0])
                normalise(g)
                if g:
                    add_logits(g - 1)
                    add_attention(g - 1)
                    stats_of(g - 1, SPLIT_DVE[g][1])
                else:
                    split(SPLIT_DVE[g][1])
                if g == 2:
                    route(0)
                    scale_logits(0)
            split(len(todo))
            add_logits(GROUPS - 1)
            route(1)
            add_attention(GROUPS - 1)

            dve.wait_ge(rank_ready, 1)
            g = GROUPS - 1
            mark(nc.vector.tensor_tensor_scan(upto[:, :], not_first[:, :], ps_total, 0.0, ALU.mult, ALU.add))
            tile_stats(g, 0)
            until_marked()
            counts = upto[:, :].rearrange("p (e t) -> p e t", e=E)[:, :, TILES - 1:TILES]
            nc.vector.tensor_tensor(more[:, :, :], counts.to_broadcast([P, E, TILES - 1]),
                                    steps128[:, :].unsqueeze(1).to_broadcast([P, E, TILES - 1]), ALU.is_gt)
            mark(nc.vector.tensor_tensor(place[:, :], upto[:, :], ps_total, ALU.subtract))
            tile_stats(g, 1)
            until_marked()
            mark(nc.vector.reduce_sum(extra[:, :], more[:, :, :], AXX))
            nc.vector.tensor_tensor(place[:, :], place[:, :], ps_rank, ALU.add)
            tile_stats(g, 2)
            until_marked()
            nc.vector.tensor_tensor_scan(last[:, :], ones8[:, :], extra[:, :], 0.0, ALU.add, ALU.add)
            mark(tile_stats(g, 3))
            until_marked()
            for j in range(GT):
                tile_mean(g, j)
            link(nc.vector.scalar_tensor_tensor(base[:, :], last[:, :], -1.0, extra[:, :], ALU.add, ALU.subtract))
            add_eps(g)
            place3 = place[:, :].rearrange("p (e t) -> p e t", e=E)
            link(nc.vector.scalar_tensor_tensor(place3, base[:, :].unsqueeze(2).to_broadcast([P, E, TILES]), float(P),
                                                place3, ALU.mult, ALU.add))
            link(nc.vector.tensor_tensor(place3, place3, chosen[:, :, :], ALU.mult))
            with nc.allow_low_precision(reason="a sum of integers below 2^24, one of them not zero"):
                link(nc.vector.reduce_sum(pos[:, :], place3.rearrange("p e t -> p t e"), AXX))
            scale_logits(1)
            link(nc.vector.tensor_scalar(pos_row[:, :], pos[:, :], P - 1, None, ALU.bitwise_and))
            nc.vector.tensor_copy(pos_rowf[:, :], pos_row[:, :]).then_inc(slot_ready, 1)
            link(nc.vector.tensor_scalar(pos_slot[:, :], pos[:, :], P.bit_length() - 1, None, ALU.logical_shift_right))
            nc.vector.tensor_tensor(slot_eq[:, :, :], iota_s[:, :].unsqueeze(1).to_broadcast([P, TILES, ST]),
                                    pos_slot[:, :].unsqueeze(2).to_broadcast([P, TILES, ST]), ALU.is_equal
                                    ).then_inc(slot_ready, 1)
            largest_prob(1)
            for t in range(DVE_ONEHOTS):
                nc.vector.tensor_scalar(row_onehot[:, t, :], iota_r[:, :], pos_rowf[:, t:t + 1], token1[:, t:t + 1],
                                        ALU.is_equal, ALU.mult).then_inc(onehot_ready, 1)
            link(nc.vector.tensor_tensor(done_e[:, :, :], last[0:1, :].unsqueeze(1).to_broadcast([1, ST, E]),
                                         iota_s[0:1, :].unsqueeze(2).to_broadcast([1, ST, E]), ALU.is_le))
            link(nc.vector.tensor_tensor(late_ok[:, :], last[0:1, E - 1 - len(LATE_FIRST):E - 1], late_first[:, :],
                                         ALU.is_ge))
            nc.vector.reduce_sum(in_time_f[:, :], late_ok[:, :], AXX)
            link(nc.vector.reduce_sum(slot_ef[:, :], done_e[:, :, :], AXX))
            for table, width in ((slot_w, WE), (slot_b1, FC), (slot_b2, D)):
                nc.vector.tensor_scalar(table[:, 0:SLOTS], slot_ef[:, 0:SLOTS], float(E - 1), float(width),
                                        ALU.min, ALU.mult)
                nc.vector.tensor_copy(table[:, IN_USE:IN_USE + 1], last[0:1, E - 1:E])
                ins = nc.vector.tensor_copy(table[:, IN_TIME:ST], in_time_f[:, :])
            ins.then_inc(table_ready, 1)
            dve.wait_ge(inv_ready, 1)
            nc.vector.tensor_copy(from_row[:, :], ps_inv).then_inc(index_ready, 1)
            link(nc.vector.tensor_scalar(empty[:, :], ps_inv, 0.0, FAR, ALU.is_equal, ALU.mult))
            nc.vector.scalar_tensor_tensor(to_row[:, :], ps_inv, -1.0, empty[:, :], ALU.add, ALU.add
                                           ).then_inc(index_ready, 1)

            def col(s, c, n=1):
                return gathered[:, s * ROW + c:s * ROW + c + n]

            def slot_norm(s):
                dve.wait_ge(landed, s + 1)
                if s:
                    dve.wait_ge(xlo_ready, s)
                nc.vector.tensor_scalar(xs, col(s, 0, D), col(s, MEAN), col(s, RSTD),
                                        ALU.subtract, ALU.mult).then_inc(xs_ready, 1)

            def x_low(s):
                dve.wait_ge(xhi_ready, s + 1)
                nc.vector.scalar_tensor_tensor(x_rows[s % 2][:, D:2 * D], xs, XS, x_rows[s % 2][:, 0:D],
                                               ALU.mult, ALU.subtract).then_inc(xlo_ready, 1)

            def h_split(s, half):
                q, part = s % 2, slice(half * F // 2, (half + 1) * F // 2)
                dve.wait_ge(gelu_ready, 2 * s + half + 1)
                if s >= 2:
                    dve.wait_ge(mm2_ready, s - 1)
                nc.vector.tensor_scalar(h_hi[q][:, part], h[:, part], HS, None, ALU.mult).then_inc(hhi_ready, 1)
                dve.wait_ge(hhi_ready, 2 * s + half + 1)
                nc.vector.scalar_tensor_tensor(h_lo[q][:, part], h[:, part], HS, h_hi[q][:, part],
                                               ALU.mult, ALU.subtract).then_inc(hlo_ready, 1)

            def finish(s):
                q = s % 2
                if s >= 1:
                    dve.wait_ge(out_ready, s)
                dve.wait_ge(mm2_ready, s + 1)
                nc.vector.scalar_tensor_tensor(y_sb[:, :], ps_y[q][:, 0:D], 1.0 / (HS * WS),
                                               b2_rep[:, bass.ds(b2_at[s], D)], ALU.mult, ALU.add).then_inc(y_half, 1)
                dve.wait_ge(y_half, s + 1)
                nc.vector.scalar_tensor_tensor(y_sb[:, :], ps_y[q][:, D:2 * D], 1.0 / (HS * WS), y_sb[:, :],
                                               ALU.mult, ALU.add).then_inc(y_ready, 1)
                dve.wait_ge(y_ready, s + 1)
                if s >= 2:
                    dve.wait_ge(stored[q], 16 * (s // 2))
                nc.vector.scalar_tensor_tensor(out_sb[q], y_sb[:, :], col(s, PMAX), col(s, 0, D),
                                               ALU.mult, ALU.add).then_inc(out_ready, 1)

            dve.wait_ge(table_ready, 1)
            b2_at, in_use, in_time = slot_offsets(slot_b2, mybir.EngineType.DVE, D)
            for s in range(3):
                slot_norm(s)
                x_low(s)
            h_split(0, 0)
            def step(s, late=False):
                if s + 3 < SLOTS:
                    slot_norm(s + 3)
                h_split(s, 1)
                if s >= 1:
                    finish(s - 1)
                if s + 3 < SLOTS:
                    x_low(s + 3)
                h_split(s + 1, 0)
                if late and EARLY_PIECES + s < PIECES:
                    split_lo(EARLY_PIECES + s)

            def last_step(s):
                h_split(s, 1)
                finish(s - 1)
                finish(s)

            dve.wait_ge(b2_in, 16)
            with dve.If(in_time > len(LATE_FIRST) - 1):
                steps_in_use(dve, in_use, lambda s: step(s, late=True), last_step)
            with dve.Else():
                for i in range(EARLY_PIECES, PIECES):
                    split_lo(i)
                steps_in_use(dve, in_use, step, last_step)


POOL_PIECES = (2, 6, 10, 14, 18)
SPLIT_POOL = (0, 1, 1, 1, 1, 1, 0, 0)
LATE_FIRST = (5, 9, 13)
LATE_PIECES = 4 * len(LATE_FIRST)
EARLY_PIECES = PIECES - LATE_PIECES
STATS_AHEAD = 4
FIRST_ACT = (1, 2, 3)
FIRST_DVE = (0, 0, 1, 1)
SPLIT_ACT = ((2, 2), (2, 2), (2, 2), (0, 2))
SPLIT_DVE = ((2, 1), (2, 2), (2, 1), (1, 2))
LOAD_X_AFTER = (0, 1, 2)
DVE_ONEHOTS = 11
AHEAD = 4

_INS = ["x", "ctx_1024", "L0_xattn_Wq", "L0_xattn_bq", "L0_xattn_Wk", "L0_xattn_bk", "L0_ffn_Wr", "L0_ffn_W1",
        "L0_ffn_b1", "L0_ffn_W2", "L0_ffn_b2"]


def kernel(**inputs):
    import numpy as _np
    import concourse.bacc as _bacc
    from concourse import mybir as _mybir
    from concourse.bass_utils import run_bass_kernel_spmd as _run

    nc = _bacc.Bacc("TRN2", target_bir_lowering=False, num_devices=1)
    arrays, args = {}, []
    for name in _INS:
        a = _np.ascontiguousarray(inputs[name])
        arrays[f"in_{name}_dram"] = a
        args.append(nc.dram_tensor(f"in_{name}_dram", a.shape, _mybir.dt.from_np(a.dtype), kind="ExternalInput").ap())
    args.append(nc.dram_tensor("out_0_dram", (B, S, D), F32, kind="ExternalOutput").ap())
    build(nc, *args)
    r = _run(nc, [arrays], core_ids=[0])
    return r.results[0]["out_0_dram"]
```
